# Optimizing a Trainium2 kernel written in Bass

```python
import numpy as np
import jax
import jax.numpy as jnp

def _softmax(x, axis=-1):
    return jax.nn.softmax(x, axis=axis)

def _gelu(x):
    return jax.nn.gelu(x, approximate=True)

def _silu(x):
    return jax.nn.silu(x)

def _sigmoid(x):
    return jax.nn.sigmoid(x)

def _layernorm(x, axis=-1, eps=1e-05):
    m = jnp.mean(x, axis=axis, keepdims=True)
    v = jnp.var(x, axis=axis, keepdims=True)
    return (x - m) / jnp.sqrt(v + eps)

def _scatter_add(tgt, idx, src, axis=0):
    return tgt.at[idx].add(src)

def _segment_sum(src, seg, n):
    return jax.ops.segment_sum(src, seg, n)
kernel_name = 'mk_macaron_d1_jaxref_r8_8bfac5'

def setup_inputs(seed: int=0):
    np.random.seed(seed)
    _w = jnp.asarray

    def _L0_attn_setup():
        import jax, jax.numpy as jnp
        import numpy as np
        N_HEAD = 16
        POWER = 4
        key = jax.random.key(seed)
        k0, k1, k2 = jax.random.split(key, 3)
        B, T, C = (2, 256, 128)
        x = jax.random.normal(k0, (B, T, C), dtype=jnp.float32)
        W_attn = jax.random.normal(k1, (C, 3 * C), dtype=jnp.float32) * 0.02
        b_attn = jnp.zeros((3 * C,), dtype=jnp.float32)
        W_proj = jax.random.normal(k2, (C, C), dtype=jnp.float32) * 0.02
        b_proj = jnp.zeros((C,), dtype=jnp.float32)
        score_gain = jnp.asarray(4.0, dtype=jnp.float32)
        return {'x': x, 'W_attn': W_attn, 'b_attn': b_attn, 'W_proj': W_proj, 'b_proj': b_proj, 'score_gain': score_gain}
    _L0_attn_in = _L0_attn_setup()

    def _L0_ffn_setup():
        import jax, jax.numpy as jnp
        import numpy as np
        TOP_K = 2
        N_GROUP = 4
        TOPK_GROUP = 2
        ROUTED_SCALE = 2.5

        def _gate(xf, gate_w, gate_bias):
            logits = xf.astype(jnp.float32) @ gate_w.astype(jnp.float32)
            scores = jax.nn.sigmoid(logits)
            sfc = scores + gate_bias.astype(jnp.float32)[None]
            T, E = sfc.shape
            e_g = E // N_GROUP
            group_feat = sfc.reshape(T, N_GROUP, e_g)
            group_scores = jax.lax.top_k(group_feat, 2)[0].sum(axis=-1)
            _, group_idx = jax.lax.top_k(group_scores, TOPK_GROUP)
            group_mask = jax.nn.one_hot(group_idx, N_GROUP, dtype=sfc.dtype).sum(axis=1)
            score_mask = jnp.broadcast_to(group_mask[..., None], (T, N_GROUP, e_g)).reshape(T, E)
            tmp_scores = jnp.where(score_mask > 0, sfc, 0.0)
            _, topk_idx = jax.lax.top_k(tmp_scores, TOP_K)
            topk_w = jnp.take_along_axis(sfc, topk_idx, axis=-1)
            topk_w = topk_w / (topk_w.sum(axis=-1, keepdims=True) + 1e-20)
            return (topk_idx, topk_w * ROUTED_SCALE)
        key = jax.random.key(seed)
        ks = jax.random.split(key, 9)
        B, N, H, I, E, SH_I = (2, 128, 128, 64, 8, 128)
        s = lambda k, shape, scale: jax.random.normal(k, shape, jnp.float32) * scale
        return {'x': s(ks[0], (B, N, H), 1.0), 'gate_w': s(ks[1], (H, E), 0.02), 'gate_bias': s(ks[2], (E,), 0.02), 'w_gate': s(ks[3], (E, H, I), 0.02), 'w_up': s(ks[4], (E, H, I), 0.02), 'w_down': s(ks[5], (E, I, H), 0.02), 'sw_gate': s(ks[6], (H, SH_I), 0.02), 'sw_up': s(ks[7], (H, SH_I), 0.02), 'sw_down': s(ks[8], (SH_I, H), 0.02)}
    _L0_ffn_in = _L0_ffn_setup()
    _d = {'L0_attn_x': _L0_attn_in['x'], 'L0_attn_W_attn': _L0_attn_in['W_attn'], 'L0_attn_b_attn': _L0_attn_in['b_attn'], 'L0_attn_W_proj': _L0_attn_in['W_proj'], 'L0_attn_b_proj': _L0_attn_in['b_proj'], 'L0_attn_score_gain': _L0_attn_in['score_gain'], 'L0_ffn_gate_w': _L0_ffn_in['gate_w'], 'L0_ffn_gate_bias': _L0_ffn_in['gate_bias'], 'L0_ffn_w_gate': _L0_ffn_in['w_gate'], 'L0_ffn_w_up': _L0_ffn_in['w_up'], 'L0_ffn_w_down': _L0_ffn_in['w_down'], 'L0_ffn_sw_gate': _L0_ffn_in['sw_gate'], 'L0_ffn_sw_up': _L0_ffn_in['sw_up'], 'L0_ffn_sw_down': _L0_ffn_in['sw_down']}
    _x0 = _d['L0_attn_x']
    _d['L0_attn_x'] = jax.random.normal(jax.random.fold_in(jax.random.key(seed), 1), (2, 1024, 128), dtype=_x0.dtype)
    del _x0
    return _d

def reference(L0_attn_x, L0_attn_W_attn, L0_attn_b_attn, L0_attn_W_proj, L0_attn_b_proj, L0_attn_score_gain, L0_ffn_gate_w, L0_ffn_gate_bias, L0_ffn_w_gate, L0_ffn_w_up, L0_ffn_w_down, L0_ffn_sw_gate, L0_ffn_sw_up, L0_ffn_sw_down):

    def _L0_attn_ref(x, W_attn, b_attn, W_proj, b_proj, score_gain):
        import jax, jax.numpy as jnp
        import numpy as np
        N_HEAD = 16
        POWER = 4
        B, T, C = x.shape
        H = N_HEAD
        D = C // H
        qkv = x @ W_attn + b_attn
        q, k, v = jnp.split(qkv, 3, axis=-1)
        to_heads = lambda t: t.reshape(B, T, H, D).transpose(0, 2, 1, 3)
        q, k, v = (to_heads(q), to_heads(k), to_heads(v))
        s = jnp.einsum('bhtd,bhsd->bhts', q, k)
        s = s - s.mean(axis=-1, keepdims=True)
        mad = jnp.abs(s).mean(axis=-1, keepdims=True) + 1e-06
        s = s / mad * score_gain
        causal = jnp.tril(jnp.ones((T, T), dtype=bool))
        s = jnp.where(causal[None, None], s, jnp.asarray(-1000.0, s.dtype))
        r = jnp.maximum(s, 0.0) ** POWER
        att = r / (r.sum(axis=-1, keepdims=True) + 1e-06)
        y = jnp.einsum('bhts,bhsd->bhtd', att, v)
        y = y.transpose(0, 2, 1, 3).reshape(B, T, C)
        return y @ W_proj + b_proj

    def _L0_ffn_ref(x, gate_w, gate_bias, w_gate, w_up, w_down, sw_gate, sw_up, sw_down):
        import jax, jax.numpy as jnp
        import numpy as np
        TOP_K = 2
        N_GROUP = 4
        TOPK_GROUP = 2
        ROUTED_SCALE = 2.5

        def _gate(xf, gate_w, gate_bias):
            logits = xf.astype(jnp.float32) @ gate_w.astype(jnp.float32)
            scores = jax.nn.sigmoid(logits)
            sfc = scores + gate_bias.astype(jnp.float32)[None]
            T, E = sfc.shape
            e_g = E // N_GROUP
            group_feat = sfc.reshape(T, N_GROUP, e_g)
            group_scores = jax.lax.top_k(group_feat, 2)[0].sum(axis=-1)
            _, group_idx = jax.lax.top_k(group_scores, TOPK_GROUP)
            group_mask = jax.nn.one_hot(group_idx, N_GROUP, dtype=sfc.dtype).sum(axis=1)
            score_mask = jnp.broadcast_to(group_mask[..., None], (T, N_GROUP, e_g)).reshape(T, E)
            tmp_scores = jnp.where(score_mask > 0, sfc, 0.0)
            _, topk_idx = jax.lax.top_k(tmp_scores, TOP_K)
            topk_w = jnp.take_along_axis(sfc, topk_idx, axis=-1)
            topk_w = topk_w / (topk_w.sum(axis=-1, keepdims=True) + 1e-20)
            return (topk_idx, topk_w * ROUTED_SCALE)
        B, N, H = x.shape
        xf = x.reshape(-1, H)
        topk_idx, topk_w = _gate(xf, gate_w, gate_bias)
        g = jax.nn.silu(jnp.einsum('th,ehi->tei', xf, w_gate))
        u = jnp.einsum('th,ehi->tei', xf, w_up)
        experts_y = jnp.einsum('tei,eih->teh', g * u, w_down)
        masked_y = jnp.take_along_axis(experts_y, topk_idx[:, :, None], axis=1)
        y = jnp.einsum('tkh,tk->th', masked_y, topk_w.astype(x.dtype)).reshape(B, N, H)
        shared = jax.nn.silu(x @ sw_gate) * (x @ sw_up) @ sw_down
        return y + shared
    x = L0_attn_x
    x = x + 0.5 * _L0_ffn_ref(_layernorm(x, axis=-1), L0_ffn_gate_w, L0_ffn_gate_bias, L0_ffn_w_gate, L0_ffn_w_up, L0_ffn_w_down, L0_ffn_sw_gate, L0_ffn_sw_up, L0_ffn_sw_down)
    x = x + _L0_attn_ref(_layernorm(x, axis=-1), L0_attn_W_attn, L0_attn_b_attn, L0_attn_W_proj, L0_attn_b_proj, L0_attn_score_gain)
    x = x + 0.5 * _L0_ffn_ref(_layernorm(x, axis=-1), L0_ffn_gate_w, L0_ffn_gate_bias, L0_ffn_w_gate, L0_ffn_w_up, L0_ffn_w_down, L0_ffn_sw_gate, L0_ffn_sw_up, L0_ffn_sw_down)
    return x

_drawn_inputs = setup_inputs


def setup_inputs(seed=0):
    import zlib

    import numpy as np

    out = dict(_drawn_inputs(seed))
    spreads = {'L0_attn_b_attn': (0.0, 0.34), 'L0_attn_b_proj': (0.0, 0.1)}
    factors = {'L0_attn_W_attn': 3.452,
     'L0_ffn_gate_w': 8.0,
     'L0_ffn_gate_bias': 8.0,
     'L0_ffn_w_gate': 7.897,
     'L0_ffn_w_up': 7.879,
     'L0_ffn_w_down': 7.895,
     'L0_ffn_sw_gate': 8.0,
     'L0_ffn_sw_up': 8.0,
     'L0_ffn_sw_down': 8.0}
    for name, (base, spread) in spreads.items():
        noise = np.random.default_rng([zlib.crc32(name.encode()), seed]).standard_normal(out[name].shape)
        drawn = base * np.exp(spread * noise) if base else spread * noise
        out[name] = jnp.asarray(drawn.astype(out[name].dtype))
    for name, factor in factors.items():
        out[name] = (out[name] * factor).astype(out[name].dtype)
    return out
```

```python
from contextlib import ExitStack

import concourse.bass as bass
from concourse import mybir

F32 = mybir.dt.float32
BF16 = mybir.dt.bfloat16
ALU = mybir.AluOpType
ACT = mybir.ActivationFunctionType

P = 128
B, T, C = 2, 1024, 128
N_HEAD = 16
D = C // N_HEAD
N = B * T
NT = N // P
SPAN = 512
NSPAN = N // SPAN
TPS = SPAN // P
E, I = 8, 64
NCH = E * I // P
HCH = NCH + 1
EPS = 1e-5

PARTS = 3
KROWS = PARTS * PARTS * D
G = 4
NQUAD = B * N_HEAD // G
QPB = NQUAD // B
NB = T // P
ROUNDS = [(0, None), (1, 7), (2, 6), (3, 5), (4, None)]
NR = len(ROUNDS)
STEPS = NR * G


def width(block):
    return T - block * P


def tile_blocks(r):
    main, extra = ROUNDS[r]
    out = [(main, main * P, main * P)]
    if extra is not None:
        out.append((extra, 0, extra * P))
    return out


def tile_low(r):
    main, extra = ROUNDS[r]
    return 0 if extra is not None else main * P


def bank_pieces(lo, hi):
    return [(a, b) for a, b in ((lo, min(hi, SPAN)), (max(lo, SPAN), hi)) if a < b]


def upper_by_vector(r, g):
    return g % 2 == 1


def square_by_gpsimd(r, g):
    return g < 3


class Chain:

    def __init__(self, engine, sem):
        self.engine, self.sem, self.n = engine, sem, 0

    def __call__(self, instruction):
        self.n += 1
        instruction.then_inc(self.sem, 1)
        self.engine.wait_ge(self.sem, self.n)


def build(nc, x_in, w_attn, b_attn, w_proj, b_proj, score_gain, gate_w, gate_bias,
          w_gate, w_up, w_down, sw_gate, sw_up, sw_down, out):
    ctx = ExitStack()
    with ctx:
        def sb(name, shape, dt=F32):
            return ctx.enter_context(nc.sbuf_tensor(name, shape, dt))

        def sem(name):
            return ctx.enter_context(nc.semaphore(name))

        m = type("Memory", (), {})()
        m.X = sb("X", [P, NT, C])
        m.xnT = sb("xnT", [P, N])
        m.WG = sb("WG", [P, HCH * P])
        m.WU = sb("WU", [P, HCH * P])
        m.WD = sb("WD", [P, HCH, C])
        m.WA = sb("WA", [P, 3 * C])
        m.WP = sb("WP", [P, C])
        m.gw = sb("gw", [P, E])
        m.gb = sb("gb", [P, E])
        m.bqk = sb("bqk", [P, 2])
        m.bv = sb("bv", [P, C])
        m.bp = sb("bp", [P, C])
        m.gain = sb("gain", [P, 1])
        m.ident = sb("ident", [P, P])
        m.identb = sb("identb", [P, P], BF16)
        m.sel = sb("sel", [P, NCH * P], BF16)
        m.ones_rows = sb("ones_rows", [P, 32])
        m.V = sb("V", [P, NQUAD, NB, G * D])
        m.upper = sb("upper", [P, NB, B * N_HEAD])
        m.arena = sb("arena", [P, 40 * 1024])
        m.psum = [ctx.enter_context(nc.psum_tensor(f"bank{i}", [P, 2 * SPAN], F32)) for i in range(4)]

        q_dram = nc.dram_tensor("q_parts", [B * N_HEAD, KROWS, T], BF16, kind="Internal").ap()
        k_dram = nc.dram_tensor("k_parts", [B * N_HEAD, PARTS * D, T], BF16, kind="Internal").ap()
        att_dram = nc.dram_tensor("att", [B * N_HEAD, 4, D, T], F32, kind="Internal").ap()

        load_and_constants(nc, m, sem, x_in, w_attn, b_attn, w_proj, b_proj, score_gain, gate_w,
                           gate_bias, w_gate, w_up, w_down, sw_gate, sw_up, sw_down)
        ffn(nc, m, sem, "f1")
        project_qkv(nc, m, sem, q_dram, k_dram)
        attention(nc, m, sem, q_dram, k_dram, att_dram)
        merge_heads(nc, m, sem, att_dram)
        ffn(nc, m, sem, "f2")
        store(nc, m, sem, out)


class Arena:

    def __init__(self, m):
        self.flat, self.at = m.arena, 0

    def take(self, n, dt=F32):
        words = n if dt == F32 else n // 2
        view = self.flat[:, self.at:self.at + words]
        self.at += words
        assert self.at <= self.flat.shape[1], self.at
        return view if dt == F32 else view.bitcast(dt)


def load_and_constants(nc, m, sem, x_in, w_attn, b_attn, w_proj, b_proj, score_gain, gate_w,
                       gate_bias, w_gate, w_up, w_down, sw_gate, sw_up, sw_down):
    loaded, made = sem("loaded"), sem("constants_made")
    x_v = x_in.rearrange("b (n p) c -> p (b n) c", p=P)
    row = lambda v: v.rearrange("(a n) -> a n", a=1)
    with nc.Block() as block:
        @block.sync
        def _(sp):
            sp.dma_start(m.X[:, :, :], x_v).then_inc(loaded, 16)
            sp.dma_start(m.gw[:, :], gate_w).then_inc(loaded, 16)
            sp.dma_start(m.gb[:, :], row(gate_bias).to_broadcast([P, E])).then_inc(loaded, 16)
            sp.dma_start(m.WG[:, 0:E * I].rearrange("h (e i) -> h e i", e=E),
                         w_gate.rearrange("e h i -> h e i")).then_inc(loaded, 16)
            sp.dma_start(m.WU[:, 0:E * I].rearrange("h (e i) -> h e i", e=E),
                         w_up.rearrange("e h i -> h e i")).then_inc(loaded, 16)
            sp.dma_start(m.WD[:, 0:NCH, :], w_down.rearrange("(c e) i h -> (e i) c h", e=E // NCH))\
                .then_inc(loaded, 16)
            sp.dma_start(m.WD[:, NCH, :], sw_down).then_inc(loaded, 16)
            sp.wait_ge(loaded, 16 * 16)

        @block.scalar
        def _(act):
            act.dma_start(m.WG[:, E * I:], sw_gate).then_inc(loaded, 16)
            act.dma_start(m.WU[:, E * I:], sw_up).then_inc(loaded, 16)
            act.dma_start(m.WA[:, :], w_attn).then_inc(loaded, 16)
            act.dma_start(m.WP[:, :], w_proj).then_inc(loaded, 16)
            act.dma_start(m.bqk[:, 0:1], b_attn[0:C].rearrange("(p a) -> p a", a=1)).then_inc(loaded, 16)
            act.dma_start(m.bqk[:, 1:2], b_attn[C:2 * C].rearrange("(p a) -> p a", a=1)).then_inc(loaded, 16)
            act.dma_start(m.bv[:, :], row(b_attn[2 * C:3 * C]).to_broadcast([P, C])).then_inc(loaded, 16)
            act.dma_start(m.bp[:, :], row(b_proj).to_broadcast([P, C])).then_inc(loaded, 16)
            act.dma_start(m.gain[:, :], score_gain.to_broadcast([P, 1])).then_inc(loaded, 16)

        @block.gpsimd
        def _(pool):
            link = Chain(pool, made)
            nc.gpsimd.memset(m.ident[:, :], 0.0).then_inc(made, 1)
            nc.gpsimd.memset(m.identb[:, :], 0.0).then_inc(made, 1)
            nc.gpsimd.memset(m.sel[:, :], 0.0).then_inc(made, 1)
            nc.gpsimd.memset(m.ones_rows[:, :], 0.0).then_inc(made, 1)
            link.n = 4
            pool.wait_ge(made, 4)
            for t in (m.ident, m.identb):
                link(nc.gpsimd.affine_select(out=t[:, :], in_=t[:, :], compare_op=ALU.not_equal, fill=1.0,
                                             base=0, pattern=[[-1, P]], channel_multiplier=1))
            for part in range(PARTS):
                link(nc.gpsimd.affine_select(out=m.sel[:, :], in_=m.sel[:, :], compare_op=ALU.not_equal,
                                             fill=1.0, base=-E * part, pattern=[[-1, E], [0, I]],
                                             channel_multiplier=1))
            link(nc.gpsimd.memset(m.ones_rows[:, 2 * D:3 * D], 1.0))


def layer_norm(nc, m, sem, tag, a, extra_tensor=None):
    s = type("Norm", (), {})()
    s.xn = a.take(NT * C).rearrange("p (n c) -> p n c", n=NT)
    s.stats = a.take(NT * 6).rearrange("p (n k) -> p n k", n=NT)
    s.mv = a.take(NT * 2).rearrange("p (n k) -> p n k", n=NT)
    s.std = a.take(NT)
    s.rstd = a.take(NT)
    s.var_ready, s.std_ready = sem(tag + "_var_ready"), sem(tag + "_std_ready")
    s.xn_ready, s.xt_ready, s.xnT_ready = sem(tag + "_xn_ready"), sem(tag + "_xt_ready"), sem(tag + "_xnT_ready")
    return s


def norm_vector(nc, m, s, dve, link):
    for t in range(NT):
        last = nc.vector.bn_stats(s.stats[:, t, :], m.X[:, t, :])
    link(last)
    for t in range(NT):
        last = nc.vector.bn_aggr(s.mv[:, t, :], s.stats[:, t, :])
    link(last)
    nc.vector.tensor_scalar(s.std, s.mv[:, :, 1], EPS, None, ALU.add).then_inc(s.var_ready, 1)
    dve.wait_ge(s.std_ready, 1)
    link(nc.vector.reciprocal(s.rstd, s.std))
    for t in range(NT):
        nc.vector.tensor_scalar(s.xn[:, t, :], m.X[:, t, :], s.mv[:, t, 0:1], s.rstd[:, t:t + 1],
                                ALU.subtract, ALU.mult).then_inc(s.xn_ready, 1)


def norm_scalar(nc, m, s, act):
    act.wait_ge(s.var_ready, 1)
    nc.scalar.activation(s.std, s.std, ACT.Sqrt).then_inc(s.std_ready, 1)
    for i in range(NSPAN):
        act.wait_ge(s.xt_ready, i + 1)
        nc.scalar.activation(m.xnT[:, i * SPAN:(i + 1) * SPAN], m.psum[i % 2][:, 0:SPAN],
                             ACT.Copy).then_inc(s.xnT_ready, 1)


def norm_tensor(nc, m, s, pe):
    for i in range(NSPAN):
        if i >= 2:
            pe.wait_ge(s.xnT_ready, i - 1)
        for k in range(TPS):
            t = i * TPS + k
            pe.wait_ge(s.xn_ready, t + 1)
            last = nc.tensor.transpose(m.psum[i % 2][:, k * P:(k + 1) * P], s.xn[:, t, :], m.ident[:, :])
        last.then_inc(s.xt_ready, 1)


def ffn(nc, m, sem, tag):
    a = Arena(m)
    s = layer_norm(nc, m, sem, tag, a)
    tile8 = lambda k=E: a.take(NT * k).rearrange("p (n e) -> p n e", n=NT)
    ex, score, kept, rank, beat, weight, rest, mid32 = (tile8() for _ in range(8))
    gsum, grank, gbeat = (tile8(E // 2) for _ in range(3))
    wsum, winv = a.take(NT), a.take(NT)
    parts = a.take(NT * PARTS * E, BF16).rearrange("p (n k e) -> p n k e", n=NT, k=PARTS)
    wT = a.take(N, BF16)
    silu = a.take(2 * SPAN).rearrange("p (k n) -> p k n", k=2)
    hid = a.take(3 * SPAN).rearrange("p (k n) -> p k n", k=3)
    HID = [0, 1, 2, 0, 1]
    USED = [0, -1, 1, 2, 3]
    yT = a.take(SPAN)
    link_sem = sem(tag + "_vector_chain")
    logits_ready, ex_ready = sem(tag + "_logits_ready"), sem(tag + "_ex_ready")
    parts_ready, wt_ready = sem(tag + "_parts_ready"), sem(tag + "_wt_ready")
    wT_zeroed, wT_ready = sem(tag + "_wT_zeroed"), sem(tag + "_wT_ready")
    gate_ready, up_ready, spread_ready = sem(tag + "_gate"), sem(tag + "_up"), sem(tag + "_spread")
    silu_ready, hid_ready = sem(tag + "_silu"), sem(tag + "_hid")
    prod_ready = sem(tag + "_prod")
    down_done, y_ready = sem(tag + "_down"), sem(tag + "_y")
    yt_ready, x_added = sem(tag + "_yt"), sem(tag + "_x")
    b = m.psum
    gate_ps = [b[0][:, 0:SPAN], b[0][:, SPAN:]]
    up_ps = [b[1][:, 0:SPAN], b[1][:, SPAN:]]
    spread_ps = [b[2][:, 0:SPAN], b[2][:, SPAN:]]
    down_ps, back_ps = b[3][:, 0:SPAN], b[3][:, SPAN:]
    logit_ps = b[2][:, 0:NT * E]
    wt_ps = b[3][:, :].bitcast(BF16)

    with nc.Block() as block:
        @block.tensor
        def _(pe):
            norm_tensor(nc, m, s, pe)
            for t in range(NT):
                pe.wait_ge(s.xnT_ready, t // TPS + 1)
                last = nc.tensor.matmul(logit_ps[:, t * E:(t + 1) * E], m.xnT[:, t * P:(t + 1) * P],
                                        m.gw[:, :], start=True, stop=True)
            last.then_inc(logits_ready, 1)
            pe.wait_ge(parts_ready, 1)
            for t in range(NT):
                last = nc.tensor.transpose(wt_ps[0:PARTS * E, t * P:(t + 1) * P],
                                           parts[:, t, :, :].rearrange("p k e -> p (k e)"), m.identb[:, :])
            last.then_inc(wt_ready, 1)
            pe.wait_ge(wT_ready, 1)

            def down(i, c, first):
                if c == NCH:
                    pe.wait_ge(prod_ready, i * HCH + HCH)
                else:
                    pe.wait_ge(hid_ready, i * NCH + c + 1)
                if c == 0 and not first:
                    pe.wait_ge(y_ready, i)
                mm = nc.tensor.matmul(down_ps, m.WD[:, c, :], hid[:, HID[c], :], start=(c == 0), stop=(c == NCH))
                if c == NCH:
                    mm.then_inc(down_done, 1)

            def turn_back(n):
                pe.wait_ge(y_ready, n)
                for k in range(TPS):
                    last = nc.tensor.transpose(back_ps[:, k * P:(k + 1) * P], yT[:, k * P:(k + 1) * P], m.ident[:, :])
                last.then_inc(yt_ready, 1)

            def span(i, first):
                x = m.xnT[:, bass.ds(i * SPAN, SPAN)]
                for c in range(HCH):
                    again = not first or c >= 2
                    if again:
                        pe.wait_ge(silu_ready, i * HCH + USED[c])
                    nc.tensor.matmul(gate_ps[c % 2], m.WG[:, c * P:(c + 1) * P], x, start=True, stop=True)\
                        .then_inc(gate_ready, 1)
                    if again:
                        pe.wait_ge(prod_ready, i * HCH + USED[c])
                    nc.tensor.matmul(up_ps[c % 2], m.WU[:, c * P:(c + 1) * P], x, start=True, stop=True)\
                        .then_inc(up_ready, 1)
                    if c < NCH:
                        if again:
                            pe.wait_ge(hid_ready, i * NCH + (c - 1))
                        nc.tensor.matmul(spread_ps[c % 2], m.sel[:, c * P:(c + 1) * P],
                                         wT[:, bass.ds(i * SPAN, SPAN)], start=True, stop=True)\
                            .then_inc(spread_ready, 1)
                    if c >= 1:
                        down(i, c - 1, first)
                    elif not first:
                        down(i - 1, NCH, False)
                    if c == 1 and not first:
                        turn_back(i)

            span(0, True)
            with pe.Fori(1, NSPAN) as i:
                span(i, False)
            down(NSPAN - 1, NCH, False)
            turn_back(NSPAN)

        @block.scalar
        def _(act):
            norm_scalar(nc, m, s, act)
            act.wait_ge(logits_ready, 1)
            nc.scalar.activation(ex.rearrange("p n e -> p (n e)"), logit_ps, ACT.Sigmoid).then_inc(ex_ready, 1)
            act.wait_ge(wT_zeroed, 1)
            act.wait_ge(wt_ready, 1)
            nc.scalar.activation(wT[0:PARTS * E, :], wt_ps[0:PARTS * E, :], ACT.Copy).then_inc(wT_ready, 1)

            def take_out(n):
                act.wait_ge(down_done, n)
                nc.scalar.activation(yT, down_ps, ACT.Copy, scale=0.5).then_inc(y_ready, 1)

            def span(i, first):
                for c in range(HCH):
                    act.wait_ge(gate_ready, i * HCH + c + 1)
                    if not first or c >= 2:
                        act.wait_ge(prod_ready, i * HCH + USED[c])
                    nc.scalar.activation(silu[:, c % 2, :], gate_ps[c % 2], ACT.Silu).then_inc(silu_ready, 1)
                    if c == 0 and not first:
                        take_out(i)

            span(0, True)
            with act.Fori(1, NSPAN) as i:
                span(i, False)
            take_out(NSPAN)

        @block.gpsimd
        def _(pool):
            nc.gpsimd.memset(wT, 0.0).then_inc(wT_zeroed, 1)

        @block.vector
        def _(dve):
            link = Chain(dve, link_sem)
            norm_vector(nc, m, s, dve, link)
            dve.wait_ge(ex_ready, 1)
            link(nc.vector.tensor_tensor(score, ex, m.gb[:, :].unsqueeze(1).to_broadcast([P, NT, E]), ALU.add))
            link(nc.vector.tensor_tensor(gsum, score[:, :, 0:E:2], score[:, :, 1:E:2], ALU.add))
            link(nc.vector.memset(grank, 0.0))
            ng = E // 2
            for d in range(1, ng):
                beat_d = gbeat[:, :, 0:ng - d]
                link(nc.vector.tensor_tensor(beat_d, gsum[:, :, 0:ng - d], gsum[:, :, d:ng], ALU.is_ge))
                link(nc.vector.tensor_tensor(grank[:, :, d:ng], grank[:, :, d:ng], beat_d, ALU.add))
                link(nc.vector.tensor_scalar(beat_d, beat_d, -1.0, 1.0, ALU.mult, ALU.add))
                link(nc.vector.tensor_tensor(grank[:, :, 0:ng - d], grank[:, :, 0:ng - d], beat_d, ALU.add))
            link(nc.vector.tensor_scalar(grank, grank, 2.0, None, ALU.is_lt))
            for k in range(2):
                last = nc.vector.tensor_tensor(kept[:, :, k:E:2], score[:, :, k:E:2], grank, ALU.mult)
            link(last)
            link(nc.vector.memset(rank, 0.0))
            for d in range(1, E):
                beat_d = beat[:, :, 0:E - d]
                link(nc.vector.tensor_tensor(beat_d, kept[:, :, 0:E - d], kept[:, :, d:E], ALU.is_ge))
                link(nc.vector.tensor_tensor(rank[:, :, d:E], rank[:, :, d:E], beat_d, ALU.add))
                link(nc.vector.tensor_scalar(beat_d, beat_d, -1.0, 1.0, ALU.mult, ALU.add))
                link(nc.vector.tensor_tensor(rank[:, :, 0:E - d], rank[:, :, 0:E - d], beat_d, ALU.add))
            link(nc.vector.tensor_scalar(rank, rank, 2.0, None, ALU.is_lt))
            link(nc.vector.tensor_tensor(weight, score, rank, ALU.mult))
            link(nc.vector.tensor_reduce(wsum, weight, mybir.AxisListType.X, ALU.add))
            link(nc.vector.tensor_scalar(wsum, wsum, 1e-20, None, ALU.add))
            link(nc.vector.reciprocal(winv, wsum))
            link(nc.vector.tensor_scalar(winv, winv, 2.5, None, ALU.mult))
            link(nc.vector.tensor_tensor(weight, weight, winv.unsqueeze(2).to_broadcast([P, NT, E]), ALU.mult))
            link(nc.vector.tensor_copy(parts[:, :, 0, :], weight))
            link(nc.vector.tensor_tensor(rest, weight, parts[:, :, 0, :], ALU.subtract))
            link(nc.vector.tensor_copy(parts[:, :, 1, :], rest))
            nc.vector.tensor_tensor(parts[:, :, 2, :], rest, parts[:, :, 1, :], ALU.subtract).then_inc(parts_ready, 1)

            def add_to_x(n):
                dve.wait_ge(yt_ready, n)
                xs = m.X[:, bass.ds((n - 1) * TPS, TPS), :].rearrange("p n c -> p (n c)")
                nc.vector.tensor_tensor(xs, back_ps, xs, ALU.add).then_inc(x_added, 1)

            def span(i, first):
                for c in range(HCH):
                    dve.wait_ge(silu_ready, i * HCH + c + 1)
                    dve.wait_ge(up_ready, i * HCH + c + 1)
                    h = hid[:, HID[c], :]
                    nc.vector.tensor_tensor(h, silu[:, c % 2, :], up_ps[c % 2], ALU.mult).then_inc(prod_ready, 1)
                    if c < NCH:
                        dve.wait_ge(prod_ready, i * HCH + c + 1)
                        dve.wait_ge(spread_ready, i * NCH + c + 1)
                        nc.vector.tensor_tensor(h, h, spread_ps[c % 2], ALU.mult).then_inc(hid_ready, 1)
                    if c == 2 and not first:
                        add_to_x(i)

            span(0, True)
            with dve.Fori(1, NSPAN) as i:
                span(i, False)
            add_to_x(NSPAN)


def project_qkv(nc, m, sem, q_dram, k_dram):
    a = Arena(m)
    s = layer_norm(nc, m, sem, "qkv", a)
    full = {"q": a.take(N), "k": a.take(N)}
    rest = a.take(N)
    parts = {w: [a.take(N, BF16) for _ in range(PARTS)] for w in "qk"}
    sign, neg = a.take(1), a.take(1)
    ksum, kmean = a.take(NSPAN), a.take(B)
    chain, rows_ready, full_ready = sem("qkv_chain"), sem("qkv_rows"), sem("qkv_out")
    v_ready, v_out = sem("v_rows"), sem("v_out")
    part_a, part_v, stored = sem("part_scalar"), sem("part_vector"), sem("parts_stored")
    rest_ready = sem("rest_ready")
    banks = [m.psum[i // 2][:, (i % 2) * SPAN:(i % 2 + 1) * SPAN] for i in range(8)]
    with nc.Block() as block:
        @block.tensor
        def _(pe):
            norm_tensor(nc, m, s, pe)
            pe.wait_ge(s.xnT_ready, NSPAN)
            for n in range(2 * NSPAN):
                w, i = n // NSPAN, n % NSPAN
                if n >= 4:
                    pe.wait_ge(full_ready, n - 3)
                nc.tensor.matmul(banks[n % 4], m.WA[:, w * C:(w + 1) * C], m.xnT[:, i * SPAN:(i + 1) * SPAN],
                                 start=True, stop=True).then_inc(rows_ready, 1)
            for i in range(NSPAN):
                for k in range(TPS):
                    t = i * TPS + k
                    last = nc.tensor.matmul(banks[4 + i][:, k * P:(k + 1) * P], m.xnT[:, t * P:(t + 1) * P],
                                            m.WA[:, 2 * C:], start=True, stop=True)
                last.then_inc(v_ready, 1)

        @block.scalar
        def _(act):
            norm_scalar(nc, m, s, act)
            act.wait_ge(full_ready, NSPAN)
            nc.scalar.activation(parts["q"][0], full["q"], ACT.Copy).then_inc(part_a, 1)
            act.wait_ge(rest_ready, 1)
            nc.scalar.activation(parts["q"][1], rest, ACT.Copy).then_inc(part_a, 1)
            act.wait_ge(full_ready, 2 * NSPAN + B)
            nc.scalar.activation(parts["k"][0], full["k"], ACT.Copy).then_inc(part_a, 1)
            act.wait_ge(rest_ready, 2)
            nc.scalar.activation(parts["k"][1], rest, ACT.Copy).then_inc(part_a, 1)

        @block.vector
        def _(dve):
            link = Chain(dve, chain)
            norm_vector(nc, m, s, dve, link)
            link(nc.vector.tensor_scalar(sign, m.gain[:, :], 0.0, None, ALU.is_gt))
            link(nc.vector.tensor_scalar(neg, m.gain[:, :], 0.0, None, ALU.is_lt))
            link(nc.vector.tensor_tensor(sign, sign, neg, ALU.subtract))
            for i in range(NSPAN):
                dve.wait_ge(rows_ready, i + 1)
                nc.vector.tensor_scalar(full["q"][:, i * SPAN:(i + 1) * SPAN], banks[i % 4], m.bqk[:, 0:1],
                                        sign[:, 0:1], ALU.add, ALU.mult).then_inc(full_ready, 1)
            for i in range(NSPAN):
                dve.wait_ge(rows_ready, NSPAN + i + 1)
                nc.vector.tensor_scalar(full["k"][:, i * SPAN:(i + 1) * SPAN], banks[i % 4], m.bqk[:, 1:2],
                                        0.0, ALU.add, ALU.add, accum_out=ksum[:, i:i + 1])\
                    .then_inc(full_ready, 1)
            dve.wait_ge(full_ready, 2 * NSPAN)
            spb = NSPAN // B
            for b in range(B):
                link(nc.vector.tensor_tensor(kmean[:, b:b + 1], ksum[:, spb * b:spb * b + 1],
                                             ksum[:, spb * b + 1:spb * b + 2], ALU.add))
            link(nc.vector.tensor_scalar(kmean, kmean, -1.0 / T, None, ALU.mult))
            for b in range(B):
                kb = full["k"][:, b * T:(b + 1) * T]
                nc.vector.tensor_scalar(kb, kb, kmean[:, b:b + 1], None, ALU.add).then_inc(full_ready, 1)
            for i in range(NSPAN):
                dve.wait_ge(v_ready, i + 1)
                b, n0 = i * TPS // NB, i * TPS % NB
                qn = lambda v: v.rearrange("p n (q c) -> p q n c", q=QPB)
                nc.vector.tensor_tensor(m.V[:, b * QPB:(b + 1) * QPB, n0:n0 + TPS, :],
                                        qn(banks[4 + i].rearrange("p (n c) -> p n c", n=TPS)),
                                        qn(m.bv[:, :].unsqueeze(1).to_broadcast([P, TPS, C])),
                                        ALU.add).then_inc(v_out, 1)
            for n, w in enumerate("qk"):
                dve.wait_ge(full_ready, 2 * NSPAN + B)
                dve.wait_ge(part_a, 2 * n + 1)
                if n:
                    dve.wait_ge(part_v, n)
                    dve.wait_ge(part_a, 2 * n)
                nc.vector.tensor_tensor(rest, full[w], parts[w][0], ALU.subtract).then_inc(rest_ready, 1)
                dve.wait_ge(rest_ready, n + 1)
                dve.wait_ge(part_a, 2 * n + 2)
                nc.vector.tensor_tensor(parts[w][2], rest, parts[w][1], ALU.subtract).then_inc(part_v, 1)

        @block.sync
        def _(sp):
            qv = q_dram.rearrange("(x h) (a b d) t -> x a b h d t", x=B, a=PARTS, b=PARTS)
            kv = k_dram.rearrange("(x h) (b d) t -> x b h d t", x=B, b=PARTS)
            n = 0
            for part in range(PARTS):
                if part < 2:
                    sp.wait_ge(part_a, part + 1)
                else:
                    sp.wait_ge(part_v, 1)
                for rep in range(PARTS):
                    for x in range(B):
                        sp.dma_start(qv[x, part, rep], parts["q"][part][:, x * T:(x + 1) * T]).then_inc(stored, 16)
                        n += 16
            for part in range(PARTS):
                if part < 2:
                    sp.wait_ge(part_a, 2 + part + 1)
                else:
                    sp.wait_ge(part_v, 2)
                for x in range(B):
                    sp.dma_start(kv[x, part], parts["k"][part][:, x * T:(x + 1) * T]).then_inc(stored, 16)
                    n += 16
            sp.wait_ge(stored, n)


def attention(nc, m, sem, q_dram, k_dram, att_dram):
    a = Arena(m)
    Q = [a.take(G * T, BF16).rearrange("p (g t) -> p g t", g=G) for _ in range(2)]
    K = [a.take(G * T, BF16).rearrange("p (g t) -> p g t", g=G) for _ in range(2)]
    masks = a.take((NR - 1) * T, BF16).rearrange("p (r t) -> p r t", r=NR - 1)
    Vq = a.take(NB * G * 32).rearrange("p (n g k) -> p n g k", n=NB, g=G)
    wide_tile = lambda: a.take(G * T).rearrange("p (g t) -> p g t", g=G)
    half_tile = lambda: a.take(G * SPAN).rearrange("p (g t) -> p g t", g=G)
    relus, powers = [wide_tile() for _ in range(2)], [wide_tile() for _ in range(NR - 1)] + [half_tile()]
    relus = [relus[0], relus[1], relus[0], relus[1], half_tile()]
    Y = lambda r, g: relus[r][:, g, :]
    Z = lambda r, g: powers[r][:, g, :]
    off = lambda r: SPAN if r == NR - 1 else 0
    sums = a.take(T)
    tiles = m.psum[0:3]
    acc = m.psum[3]

    prep, chain = sem("att_prep"), sem("att_chain")
    qk_loaded = [sem("qk_loaded0"), sem("qk_loaded1")]
    lower_ready, upper_ready = sem("lower_ready"), sem("upper_ready")
    relu_done, square_done = sem("relu_done"), sem("square_done")
    upper_v, upper_a = sem("upper_summed_vector"), sem("upper_summed_scalar")
    fourth_p, fourth_a = sem("fourth_gpsimd"), sem("fourth_scalar")
    sums_out, sums_stored = sem("sums_out"), sem("sums_stored")
    power_summed, relu_summed = sem("power_round_summed"), sem("relu_round_summed")
    sums_free = sem("sums_free")
    vq_ready = sem("vq_ready")
    steps = [(r, g) for r in range(NR) for g in range(G)]
    count = lambda who, upto, inclusive=True: sum(who(r, g) for r, g in steps[:steps.index(upto) + inclusive])
    all_of = lambda who: sum(who(r, g) for r, g in steps)
    by_v, by_a = upper_by_vector, lambda r, g: not upper_by_vector(r, g)
    sq_p, sq_a = square_by_gpsimd, lambda r, g: not square_by_gpsimd(r, g)
    NV, NA, NP4, NA4 = all_of(by_v), all_of(by_a), all_of(sq_p), all_of(sq_a)
    QK_DMAS = 1 + PARTS
    order = []
    for r, g in steps:
        order += [("both", r, g)] if r == NR - 1 else [("lower", r, g), ("upper", r, g)]
    assert len(order) % 3 == 0
    slot = {}
    for n, (kind, r, g) in enumerate(order):
        for k in ("lower", "upper") if kind == "both" else (kind,):
            slot[k, r, g] = n % 3

    def quads(engine, body):
        body(0, 0, 1)
        with engine.Fori(0, NQUAD // 2 - 1) as pair:
            body(2 * pair + 1, 1, pair + 1)
            body(2 * pair + 2, 0, pair + 2)
        body(NQUAD - 1, 1, NQUAD // 2)

    first_quad = lambda q: isinstance(q, int) and q == 0
    last_quad = lambda q: isinstance(q, int) and q == NQUAD - 1

    with nc.Block() as block:
        @block.sync
        def _(sp):
            def load(q, buf):
                rows = q_dram[bass.ds(q * G, G)].rearrange("h r t -> r h t")
                sp.dma_start(Q[buf][0:KROWS, :, :], rows).then_inc(qk_loaded[buf], 16)
                rows = k_dram[bass.ds(q * G, G)].rearrange("h r t -> r h t")
                for rep in range(PARTS):
                    lo = rep * PARTS * D
                    sp.dma_start(K[buf][lo:lo + PARTS * D, :, :], rows).then_inc(qk_loaded[buf], 16)

            def store(n):
                sp.wait_ge(sums_out, n)
                for g in range(G):
                    head = att_dram[bass.ds((n - 1) * G + g, 1)].rearrange("h k d t -> (h k d) t")
                    sp.dma_start(head, sums[32 * g:32 * (g + 1), :]).then_inc(sums_stored, 16)
                sp.wait_ge(sums_stored, 16 * G * n)
                sp.sem_inc(sums_free, 1)

            def body(q, buf, nth):
                if not last_quad(q):
                    if not first_quad(q):
                        sp.wait_ge(upper_ready, q * STEPS)
                    load(q + 1, 1 - buf)
                if not first_quad(q):
                    store(q)

            sp.sem_inc(sums_free, 1)
            sp.wait_ge(prep, 4)
            load(0, 0)
            quads(sp, body)
            store(NQUAD)

        @block.tensor
        def _(pe):
            def wait_tile(q, r, g, kind):
                n = next(i for i, (k, rr, gg) in enumerate(order) if (rr, gg) == (r, g) and k in (kind, "both"))
                back = n - 3
                if back < 0 and first_quad(q):
                    return
                k, rr, gg = order[back]
                qq = q - 1 if back < 0 else q
                at = (rr, gg)
                if k in ("lower", "both"):
                    pe.wait_ge(relu_done, qq * STEPS + steps.index(at) + 1)
                if k in ("upper", "both"):
                    if by_v(*at):
                        pe.wait_ge(upper_v, qq * NV + count(by_v, at))
                    else:
                        pe.wait_ge(upper_a, qq * NA + count(by_a, at))

            def fill(q, par, r, g, kind):
                left, right = (K, Q) if kind == "lower" else (Q, K)
                bank = tiles[slot[kind, r, g]]
                shift = -SPAN if (r == NR - 1 and kind == "upper") else 0
                for blk, col, seq in tile_blocks(r):
                    for lo, hi in bank_pieces(col, col + width(blk)):
                        s0 = seq + lo - col
                        last = nc.tensor.matmul(bank[:, lo + shift:hi + shift], left[par][:, g, blk * P:(blk + 1) * P],
                                                right[par][:, g, s0:s0 + hi - lo], start=True, stop=True)
                last.then_inc(lower_ready if kind == "lower" else upper_ready, 1)

            def pieces(q, what, r):
                skip = P if what == "relu" else 0
                cut = [(blk, lo, hi, seq - col) for blk, col, seq in tile_blocks(r)
                       for lo, hi in bank_pieces(col + skip, col + width(blk))]
                return [(q, what, r, n == 0, n == len(cut) - 1, *c) for n, c in enumerate(cut)]

            def add_piece(q, what, r, first, last, blk, lo, hi, to_seq):
                if first and what == "relu":
                    pe.wait_ge(relu_done, q * STEPS + (r + 1) * G)
                    if r == 0 and not first_quad(q):
                        pe.wait_ge(sums_out, q)
                if first and what == "power":
                    pe.wait_ge(fourth_p, q * NP4 + count(sq_p, (r, G - 1)))
                    pe.wait_ge(fourth_a, q * NA4 + count(sq_a, (r, G - 1)))
                    if r == 0:
                        pe.wait_ge(vq_ready, q + 1)
                s0 = lo + to_seq
                start = what == "relu" and r == 0
                stop = what == "power" and (r == NR - 1 or (r == NR - 2 and s0 < SPAN))
                for g in range(G):
                    src = (Z if what == "power" else Y)(r, g)[:, lo - off(r):hi - off(r)]
                    w = Vq[:, blk, g, :] if what == "power" else m.ones_rows[:, :]
                    mm = nc.tensor.matmul(acc[32 * g:32 * (g + 1), s0:s0 + hi - lo], w, src, start=start,
                                          stop=stop, skip_group_check=True)
                if last:
                    mm.then_inc(relu_summed if what == "relu" else power_summed, 1)

            def plan(q, r):
                last = [] if first_quad(q) else [q - 1]
                some = lambda quad, what, rr: [x for p in quad for x in pieces(p, what, rr)]
                if r == 1:
                    return [some(last, "power", 4), [], some([q], "relu", 0), []]
                work = {0: some(last, "relu", 3) + some(last, "power", 3) + some(last, "relu", 4),
                        2: some([q], "power", 0) + some([q], "relu", 1),
                        3: some([q], "power", 1) + some([q], "relu", 2),
                        4: some([q], "power", 2)}[r]
                return [work[g * len(work) // G:(g + 1) * len(work) // G] for g in range(G)]

            def body(q, buf, nth):
                pe.wait_ge(qk_loaded[buf], nth * (16 * QK_DMAS))
                for r, g in steps:
                    for kind in ("lower", "upper"):
                        if kind == "lower" or r < NR - 1:
                            wait_tile(q, r, g, kind)
                        fill(q, buf, r, g, kind)
                    for piece in plan(q, r)[g]:
                        add_piece(*piece)

            pe.wait_ge(prep, 4)
            quads(pe, body)
            for what, r in (("relu", 3), ("power", 3), ("relu", 4), ("power", 4)):
                for piece in pieces(NQUAD - 1, what, r):
                    add_piece(*piece)

        @block.vector
        def _(dve):
            dve.wait_ge(prep, 8)
            def body(q, buf, nth):
                for r, g in steps:
                    lo, hi = tile_low(r), T
                    before = {0: -3, 1: -2, 2: 0, 3: 1, 4: -1}[r]
                    if r in (2, 3) or not first_quad(q):
                        dve.wait_ge(relu_summed, q * NR + before + 1)
                        dve.wait_ge(square_done, (q * NR + before) * G + g + 1)
                    dve.wait_ge(lower_ready, q * STEPS + r * G + g + 1)
                    mask = masks[:, 0, 0:SPAN] if r == NR - 1 else masks[:, r, lo:hi]
                    nc.vector.scalar_tensor_tensor(Y(r, g)[:, lo - off(r):hi - off(r)],
                                                   tiles[slot["lower", r, g]][:, lo:hi], 0.0, mask,
                                                   ALU.max, ALU.mult).then_inc(relu_done, 1)
                    if by_v(r, g):
                        dve.wait_ge(upper_ready, q * STEPS + r * G + g + 1)
                        shift = -SPAN if r == NR - 1 else 0
                        for blk, col, seq in tile_blocks(r):
                            src = tiles[slot["upper", r, g]][:, col + shift:col + width(blk) + shift]
                            last = nc.vector.tensor_scalar(src, src, 0.0, 0.0, ALU.max, ALU.add,
                                                           accum_out=m.upper[:, blk, bass.ds(q * G + g, 1)])
                        last.then_inc(upper_v, 1)
            quads(dve, body)

        @block.scalar
        def _(act):
            def evacuate(n):
                act.wait_ge(power_summed, n * NR)
                act.wait_ge(sums_free, n)
                nc.scalar.activation(sums, acc[:, :], ACT.Copy).then_inc(sums_out, 1)

            def body(q, buf, nth):
                for r, g in steps:
                    if (r, g) == (1, 1) and not first_quad(q):
                        evacuate(q)
                    n = q * STEPS + r * G + g + 1
                    if by_a(r, g):
                        act.wait_ge(upper_ready, n)
                        shift = -SPAN if r == NR - 1 else 0
                        for blk, col, seq in tile_blocks(r):
                            src = tiles[slot["upper", r, g]][:, col + shift:col + width(blk) + shift]
                            last = nc.scalar.activation(src, src, ACT.Relu,
                                                        accum_out=m.upper[:, blk, bass.ds(q * G + g, 1)])
                        last.then_inc(upper_a, 1)
                    lo = tile_low(r) - off(r)
                    hi = T - off(r)
                    z = Z(r, g)[:, lo:hi]
                    if not first_quad(q):
                        act.wait_ge(power_summed, (q - 1) * NR + r + 1)
                    act.wait_ge(relu_done, n)
                    nc.scalar.activation(z, Y(r, g)[:, lo:hi], ACT.Square).then_inc(square_done, 1)
                    if sq_a(r, g):
                        act.wait_ge(square_done, n)
                        nc.scalar.activation(z, z, ACT.Square).then_inc(fourth_a, 1)
            quads(act, body)
            evacuate(NQUAD)

        @block.gpsimd
        def _(pool):
            for t in (*Q, *K):
                nc.gpsimd.memset(t[64:P, :, :], 0.0).then_inc(prep, 1)
            pool.wait_ge(prep, 4)
            nc.gpsimd.memset(masks, 1.0).then_inc(chain, 1)
            pool.wait_ge(chain, 1)
            for r in range(NR - 1):
                for blk, col, seq in tile_blocks(r):
                    d = masks[:, r, col:col + P]
                    last = nc.gpsimd.affine_select(out=d, in_=d, compare_op=ALU.is_ge, fill=0.0, base=0,
                                                   pattern=[[1, P]], channel_multiplier=-1)
                last.then_inc(prep, 1)
            nc.gpsimd.memset(Vq, 0.0).then_inc(chain, 1)
            pool.wait_ge(chain, 2)
            nc.gpsimd.memset(Vq[:, :, :, D:2 * D], 1.0).then_inc(chain, 1)

            def copy_v(q):
                src = m.V[:, bass.ds(q, 1), :, :].rearrange("p q n (g d) -> p (q n) g d", g=G)
                nc.gpsimd.tensor_copy(Vq[:, :, :, 0:D], src).then_inc(vq_ready, 1)

            def body(q, buf, nth):
                for r, g in steps:
                    if (r, g) == (1, 0) and not first_quad(q):
                        pool.wait_ge(power_summed, q * NR)
                        copy_v(q)
                    if sq_p(r, g):
                        pool.wait_ge(square_done, q * STEPS + r * G + g + 1)
                        lo = tile_low(r) - off(r)
                        hi = T - off(r)
                        z = Z(r, g)[:, lo:hi]
                        nc.gpsimd.tensor_tensor(z, z, z, ALU.mult).then_inc(fourth_p, 1)
            copy_v(0)
            quads(pool, body)


def merge_heads(nc, m, sem, att_dram):
    a = Arena(m)
    num, den, low = a.take(N), a.take(N), a.take(N)
    mad, fourth, rden = a.take(N), a.take(N), a.take(N)
    ginv = a.take(1)
    wide = a.take(NB * B * C).rearrange("p (i h d) -> p i h d", i=NB, d=D)
    wide_ready = sem("upper_wide")
    loaded, chain = sem("merge_loaded"), sem("merge_chain")
    upper_t, mad_ready, square, fourth_ready = sem("upper_t"), sem("mad_ready"), sem("mad_square"), sem("mad_fourth")
    att_ready, proj_ready, xb = sem("att_ready"), sem("proj_ready"), sem("x_bias")
    HALVES = N // T
    banks = [m.psum[i // 2][:, (i % 2) * SPAN:(i % 2 + 1) * SPAN] for i in range(8)]
    with nc.Block() as block:
        @block.sync
        def _(sp):
            v = att_dram.rearrange("(b h) k d t -> b k h d t", b=B)
            for b in range(B):
                for k, dst in ((2, low), (1, den), (0, num)):
                    sp.dma_start(dst[:, b * T:(b + 1) * T], v[b, k]).then_inc(loaded, 16)

        @block.tensor
        def _(pe):
            pe.wait_ge(wide_ready, 1)
            for b in range(B):
                for i in range(NB):
                    u = wide[:, i, b * N_HEAD:(b + 1) * N_HEAD, :].rearrange("p h d -> p (h d)")
                    last = nc.tensor.matmul(m.psum[b][:, i * P:(i + 1) * P], u, m.ident[:, :], start=True, stop=True)
                last.then_inc(upper_t, 1)
            for i in range(NSPAN):
                pe.wait_ge(att_ready, i + 1)
                for k in range(TPS):
                    t = i * TPS + k
                    last = nc.tensor.matmul(banks[4 + i][:, k * P:(k + 1) * P], rden[:, t * P:(t + 1) * P],
                                            m.WP[:, :], start=True, stop=True)
                last.then_inc(proj_ready, 1)

        @block.scalar
        def _(act):
            for b in range(B):
                sl = slice(b * T, (b + 1) * T)
                act.wait_ge(mad_ready, b + 1)
                nc.scalar.activation(fourth[:, sl], mad[:, sl], ACT.Square, scale=ginv[:, 0:1]).then_inc(square, 1)
                act.wait_ge(square, b + 1)
                nc.scalar.activation(fourth[:, sl], fourth[:, sl], ACT.Square).then_inc(fourth_ready, 1)

        @block.gpsimd
        def _(pool):
            nc.gpsimd.tensor_copy(wide.rearrange("p i h d -> p (i h) d"),
                                  m.upper[:, :, :].rearrange("p i h -> p (i h)").unsqueeze(2)
                                  .to_broadcast([P, NB * B * N_HEAD, D])).then_inc(wide_ready, 1)
            nc.gpsimd.tensor_tensor(m.X[:, :, :], m.X[:, :, :], m.bp[:, :].unsqueeze(1).to_broadcast([P, NT, C]),
                                    ALU.add).then_inc(xb, 1)

        @block.vector
        def _(dve):
            link = Chain(dve, chain)
            link(nc.vector.reciprocal(ginv, m.gain[:, :]))
            for b in range(B):
                sl = slice(b * T, (b + 1) * T)
                dve.wait_ge(upper_t, b + 1)
                dve.wait_ge(loaded, 16 * 3 * B)
                link(nc.vector.tensor_tensor(mad[:, sl], m.psum[b][:, :], low[:, sl], ALU.add))
                nc.vector.tensor_scalar(mad[:, sl], mad[:, sl], 2.0 / T, 1e-6, ALU.mult, ALU.add).then_inc(mad_ready, 1)
            for i in range(NSPAN):
                sl = slice(i * SPAN, (i + 1) * SPAN)
                dve.wait_ge(fourth_ready, i // (NSPAN // B) + 1)
                link(nc.vector.scalar_tensor_tensor(rden[:, sl], fourth[:, sl], 1e-6, den[:, sl], ALU.mult, ALU.add))
                link(nc.vector.reciprocal(rden[:, sl], rden[:, sl]))
                nc.vector.tensor_tensor(rden[:, sl], rden[:, sl], num[:, sl], ALU.mult).then_inc(att_ready, 1)
            dve.wait_ge(xb, 1)
            for i in range(NSPAN):
                dve.wait_ge(proj_ready, i + 1)
                xs = m.X[:, i * TPS:(i + 1) * TPS, :].rearrange("p n c -> p (n c)")
                last = nc.vector.tensor_tensor(xs, banks[4 + i], xs, ALU.add)
            link(last)


def store(nc, m, sem, out):
    stored = sem("x_stored")
    with nc.Block() as block:
        @block.sync
        def _(sp):
            sp.dma_start(out.rearrange("b (n p) c -> p (b n) c", p=P), m.X[:, :, :]).then_inc(stored, 16)
            sp.wait_ge(stored, 16)


_INS = ['L0_attn_x', 'L0_attn_W_attn', 'L0_attn_b_attn', 'L0_attn_W_proj', 'L0_attn_b_proj', 'L0_attn_score_gain',
        'L0_ffn_gate_w', 'L0_ffn_gate_bias', 'L0_ffn_w_gate', 'L0_ffn_w_up', 'L0_ffn_w_down', 'L0_ffn_sw_gate',
        'L0_ffn_sw_up', 'L0_ffn_sw_down']


def kernel(**inputs):
    import numpy as np
    import concourse.bacc as bacc
    from concourse.bass_utils import run_bass_kernel_spmd

    nc = bacc.Bacc("TRN2", target_bir_lowering=False, num_devices=1)
    arrays, args = {}, []
    for name in _INS:
        a = np.ascontiguousarray(inputs[name])
        if a.ndim == 0:
            a = a.reshape(1, 1)
        arrays[f"in_{name}"] = a
        args.append(nc.dram_tensor(f"in_{name}", a.shape, mybir.dt.from_np(a.dtype), kind="ExternalInput").ap())
    out = nc.dram_tensor("out_x", (B, T, C), F32, kind="ExternalOutput").ap()
    build(nc, *args, out)
    r = run_bass_kernel_spmd(nc, [arrays], core_ids=[0])
    return r.results[0]["out_x"]
```

```python
from contextlib import ExitStack

import concourse.bass as bass
from concourse import mybir

F32 = mybir.dt.float32
BF16 = mybir.dt.bfloat16
ALU = mybir.AluOpType
ACT = mybir.ActivationFunctionType

P = 128
B, T, C = 2, 1024, 128
N_HEAD = 16
D = C // N_HEAD
N = B * T
NT = N // P
SPAN = 512
NSPAN = N // SPAN
TPS = SPAN // P
E, I = 8, 64
NCH = E * I // P
HCH = NCH + 1
EPS = 1e-5

PARTS = 3
KROWS = PARTS * PARTS * D
G = 4
NQUAD = B * N_HEAD // G
QPB = NQUAD // B
NB = T // P
ROUNDS = [(0, None), (1, 7), (2, 6), (3, 5), (4, None)]
NR = len(ROUNDS)
STEPS = NR * G
QUARTERS = P // (B * N_HEAD)


def width(block):
    return T - block * P


def tile_blocks(r):
    main, extra = ROUNDS[r]
    out = [(main, main * P, main * P)]
    if extra is not None:
        out.append((extra, 0, extra * P))
    return out


def tile_low(r):
    main, extra = ROUNDS[r]
    return 0 if extra is not None else main * P


def bank_pieces(lo, hi):
    return [(a, b) for a, b in ((lo, min(hi, SPAN)), (max(lo, SPAN), hi)) if a < b]


def upper_by_vector(r, g):
    return g % 2 == 1


def square_by_gpsimd(r, g):
    return g < 3


class Chain:

    def __init__(self, engine, sem):
        self.engine, self.sem, self.n = engine, sem, 0

    def __call__(self, instruction):
        self.n += 1
        instruction.then_inc(self.sem, 1)
        self.engine.wait_ge(self.sem, self.n)


def build(nc, x_in, w_attn, b_attn, w_proj, b_proj, score_gain, gate_w, gate_bias,
          w_gate, w_up, w_down, sw_gate, sw_up, sw_down, out):
    ctx = ExitStack()
    with ctx:
        def sb(name, shape, dt=F32):
            return ctx.enter_context(nc.sbuf_tensor(name, shape, dt))

        def sem(name):
            return ctx.enter_context(nc.semaphore(name))

        m = type("Memory", (), {})()
        m.X = sb("X", [P, NT, C])
        m.xnT = sb("xnT", [P, N])
        m.WG = sb("WG", [P, HCH * P])
        m.WU = sb("WU", [P, HCH * P])
        m.WD = sb("WD", [P, HCH, C])
        m.WA = sb("WA", [P, 3 * C])
        m.WP = sb("WP", [P, C])
        m.gw = sb("gw", [P, 32])
        m.gb = sb("gb", [P, E])
        m.bqk = sb("bqk", [P, 2])
        m.bv = sb("bv", [P, C])
        m.bp = sb("bp", [P, C])
        m.gain = sb("gain", [P, 1])
        m.ident = sb("ident", [P, P])
        m.identb = sb("identb", [P, P], BF16)
        m.sel = sb("sel", [P, NCH * P], BF16)
        m.ones_rows = sb("ones_rows", [P, 32])
        m.V = sb("V", [P, NQUAD, NB, G * D])
        m.upper = sb("upper", [P, NB, B * N_HEAD])
        m.stats = sb("stats", [P, NT, 6])
        m.mv = sb("mv", [P, NT, 2])
        m.eps = sb("eps", [P, 1])
        m.table = sb("table", [P, 1])
        m.spread = sb("spread", [P, QUARTERS, B, N_HEAD * D])
        m.Q = [sb(f"Q{i}", [P, G, T], BF16) for i in range(2)]
        m.K = [sb(f"K{i}", [P, G, T], BF16) for i in range(2)]
        m.masks = sb("masks", [P, NR - 1, T], BF16)
        m.Vq = sb("Vq", [P, NB, G, 32])
        m.arena = sb("arena", [P, 29 * 1024])
        m.psum = [ctx.enter_context(nc.psum_tensor(f"bank{i}", [P, 2 * SPAN], F32)) for i in range(4)]

        q_dram = nc.dram_tensor("q_parts", [B * N_HEAD, PARTS * D, T], BF16, kind="Internal").ap()
        k_dram = nc.dram_tensor("k_parts", [B * N_HEAD, PARTS * D, T], BF16, kind="Internal").ap()
        att_dram = nc.dram_tensor("att", [B * N_HEAD, 4, D, T], F32, kind="Internal").ap()

        m.num_loaded = sem("num_loaded")
        m.weights_loaded = sem("weights_loaded")
        m.parts_stored = [sem("parts_stored0"), sem("parts_stored1")]
        m.qk_loaded = [sem("qk_loaded0"), sem("qk_loaded1")]
        load_and_constants(nc, m, sem, x_in, w_attn, b_attn, w_proj, b_proj, score_gain, gate_w,
                           gate_bias, w_gate, w_up, w_down, sw_gate, sw_up, sw_down)
        ffn(nc, m, sem, "f1", attention_constants)
        project_qkv(nc, m, sem, q_dram, k_dram)
        attention(nc, m, sem, q_dram, k_dram, att_dram)
        merge_heads(nc, m, sem, att_dram)
        ffn(nc, m, sem, "f2", None, out)


class Arena:

    def __init__(self, m):
        self.flat, self.at = m.arena, 0

    def take(self, n, dt=F32):
        words = n if dt == F32 else n // 2
        view = self.flat[:, self.at:self.at + words]
        self.at += words
        assert self.at <= self.flat.shape[1], self.at
        return view if dt == F32 else view.bitcast(dt)


WEIGHT_DMAS = 13


def load_and_constants(nc, m, sem, x_in, w_attn, b_attn, w_proj, b_proj, score_gain, gate_w,
                       gate_bias, w_gate, w_up, w_down, sw_gate, sw_up, sw_down):
    x_loaded, gate_loaded, made = [sem(f"x_loaded{i}") for i in range(NSPAN)], sem("gate_loaded"), sem("constants_made")
    gw_zeroed, stats_ready = sem("gw_zeroed"), sem("x_stats")
    x_v = x_in.rearrange("b (n p) c -> p (b n) c", p=P)
    row = lambda v: v.rearrange("(a n) -> a n", a=1)
    with nc.Block() as block:
        @block.sync
        def _(sp):
            for i in range(NSPAN):
                t = slice(i * TPS, (i + 1) * TPS)
                sp.dma_start(m.X[:, t, :], x_v[:, t, :]).then_inc(x_loaded[i], 16)
            sp.dma_start(m.WU[:, 0:E * I].rearrange("h (e i) -> h e i", e=E),
                         w_up.rearrange("e h i -> h e i")).then_inc(m.weights_loaded, 16)
            sp.dma_start(m.WD[:, 0:NCH, :], w_down.rearrange("(c e) i h -> (e i) c h", e=E // NCH))\
                .then_inc(m.weights_loaded, 16)
            sp.dma_start(m.WD[:, NCH, :], sw_down).then_inc(m.weights_loaded, 16)
            sp.dma_start(m.WU[:, E * I:], sw_up).then_inc(m.weights_loaded, 16)
            sp.wait_ge(gate_loaded, 2 * 16)

        @block.scalar
        def _(act):
            act.wait_ge(gw_zeroed, 1)
            act.dma_start(m.gw[:, 0:E], gate_w).then_inc(gate_loaded, 16)
            act.dma_start(m.gb[:, :], row(gate_bias).to_broadcast([P, E])).then_inc(gate_loaded, 16)
            act.dma_start(m.WG[:, 0:E * I].rearrange("h (e i) -> h e i", e=E),
                          w_gate.rearrange("e h i -> h e i")).then_inc(m.weights_loaded, 16)
            act.dma_start(m.WG[:, E * I:], sw_gate).then_inc(m.weights_loaded, 16)
            act.dma_start(m.WA[:, :], w_attn).then_inc(m.weights_loaded, 16)
            act.dma_start(m.WP[:, :], w_proj).then_inc(m.weights_loaded, 16)
            for n in range(2):
                act.dma_start(m.bqk[:, n:n + 1], b_attn[n * C:(n + 1) * C].rearrange("(p a) -> p a", a=1))\
                    .then_inc(m.weights_loaded, 16)
            act.dma_start(m.bv[:, :], row(b_attn[2 * C:3 * C]).to_broadcast([P, C])).then_inc(m.weights_loaded, 16)
            act.dma_start(m.bp[:, :], row(b_proj).to_broadcast([P, C])).then_inc(m.weights_loaded, 16)
            act.dma_start(m.gain[:, :], score_gain.to_broadcast([P, 1])).then_inc(m.weights_loaded, 16)

        @block.gpsimd
        def _(pool):
            nc.gpsimd.memset(m.gw[:, :], 0.0).then_inc(gw_zeroed, 1)
            nc.gpsimd.memset(m.eps[:, :], EPS).then_inc(made, 1)
            nc.gpsimd.memset(m.ident[:, :], 0.0).then_inc(made, 1)
            nc.gpsimd.memset(m.identb[:, :], 0.0).then_inc(made, 1)
            nc.gpsimd.memset(m.sel[:, :], 0.0).then_inc(made, 1)
            link = Chain(pool, made)
            link.n = 4
            for t in (m.ident, m.identb):
                pool.wait_ge(made, 4)
                link(nc.gpsimd.affine_select(out=t[:, :], in_=t[:, :], compare_op=ALU.not_equal, fill=1.0,
                                             base=0, pattern=[[-1, P]], channel_multiplier=1))
            for part in range(PARTS):
                link(nc.gpsimd.affine_select(out=m.sel[:, :], in_=m.sel[:, :], compare_op=ALU.not_equal,
                                             fill=1.0, base=-E * part, pattern=[[-1, E], [0, I]],
                                             channel_multiplier=1))

        @block.vector
        def _(dve):
            for i in range(NSPAN):
                dve.wait_ge(x_loaded[i], 16)
                span_stats(nc, m, i, stats_ready)
                span_moments(nc, m, dve, i, stats_ready)


def attention_constants(nc, m, sem, pool):
    zeroed, made = sem("operands_zeroed"), sem("attention_constants")
    for t in (*m.Q, *m.K):
        nc.gpsimd.memset(t[64:P, :, :].rearrange("p g t -> p (g t)").bitcast(F32), 0.0).then_inc(zeroed, 1)
    pool.wait_ge(zeroed, 4)
    nc.gpsimd.memset(m.ones_rows[:, :], 0.0).then_inc(made, 1)
    nc.gpsimd.memset(m.spread[:, :, :, :], 0.0).then_inc(made, 1)
    nc.gpsimd.memset(m.Vq[:, :, :, :], 0.0).then_inc(made, 1)
    nc.gpsimd.memset(m.masks[:, :, :], 1.0).then_inc(made, 1)
    link = Chain(pool, made)
    link.n = 4
    pool.wait_ge(made, 4)
    link(nc.gpsimd.memset(m.ones_rows[:, 2 * D:3 * D], 1.0))
    link(nc.gpsimd.memset(m.Vq[:, :, :, D:2 * D], 1.0))
    for n in range(QUARTERS):
        last = nc.gpsimd.affine_select(out=m.spread[:, n], in_=m.spread[:, n], compare_op=ALU.not_equal,
                                       fill=1.0, base=-B * N_HEAD * n, pattern=[[-N_HEAD, B], [-1, N_HEAD], [0, D]],
                                       channel_multiplier=1)
    for r in range(NR - 1):
        for blk, col, seq in tile_blocks(r):
            d = m.masks[:, r, col:col + P]
            last = nc.gpsimd.affine_select(out=d, in_=d, compare_op=ALU.is_ge, fill=0.0, base=0,
                                           pattern=[[1, P]], channel_multiplier=-1)
    link(last)


def span_stats(nc, m, i, stats_ready):
    for k in range(TPS):
        t = bass.ds(i * TPS + k, 1)
        last = nc.vector.bn_stats(m.stats[:, t, :].rearrange("p a k -> p (a k)"),
                                  m.X[:, t, :].rearrange("p a c -> p (a c)"))
    last.then_inc(stats_ready, 1)


def span_moments(nc, m, dve, i, stats_ready):
    dve.wait_ge(stats_ready, i + 1)
    for t in range(i * TPS, (i + 1) * TPS):
        nc.vector.bn_aggr(m.mv[:, t, :], m.stats[:, t, :])


def layer_norm(nc, m, sem, tag, a, banks):
    s = type("Norm", (), {})()
    s.xn = a.take(NT * C).rearrange("p (n c) -> p n c", n=NT)
    s.std = a.take(NT)
    s.rstd = a.take(NT)
    s.banks = banks
    s.std_ready, s.rstd_ready = sem(tag + "_std_ready"), sem(tag + "_rstd_ready")
    s.xn_ready, s.xt_ready, s.xnT_ready = sem(tag + "_xn_ready"), sem(tag + "_xt_ready"), sem(tag + "_xnT_ready")
    return s


def norm_vector(nc, m, s, dve):
    dve.wait_ge(s.std_ready, 1)
    nc.vector.reciprocal(s.rstd, s.std).then_inc(s.rstd_ready, 1)
    dve.wait_ge(s.rstd_ready, 1)
    for t in range(NT):
        nc.vector.tensor_scalar(s.xn[:, t, :], m.X[:, t, :], m.mv[:, t, 0:1], s.rstd[:, t:t + 1],
                                ALU.subtract, ALU.mult).then_inc(s.xn_ready, 1)


def norm_root(nc, m, s, act):
    nc.scalar.activation(s.std, m.mv[:, :, 1], ACT.Sqrt, bias=m.eps[:, 0:1]).then_inc(s.std_ready, 1)


def norm_take(nc, m, s, act, i):
    act.wait_ge(s.xt_ready, i + 1)
    nc.scalar.activation(m.xnT[:, i * SPAN:(i + 1) * SPAN], s.banks[i % 2], ACT.Copy).then_inc(s.xnT_ready, 1)


def norm_transpose(nc, m, s, pe, i):
    if i >= 2:
        pe.wait_ge(s.xnT_ready, i - 1)
    for k in range(TPS):
        t = i * TPS + k
        pe.wait_ge(s.xn_ready, t + 1)
        last = nc.tensor.transpose(s.banks[i % 2][:, k * P:(k + 1) * P], s.xn[:, t, :], m.ident[:, :])
    last.then_inc(s.xt_ready, 1)


def ffn(nc, m, sem, tag, beside=None, out=None):
    a = Arena(m)
    b = m.psum
    s = layer_norm(nc, m, sem, tag, a, [b[0][:, 0:SPAN], b[1][:, 0:SPAN]])
    tile8 = lambda k=E: a.take(NT * k).rearrange("p (n e) -> p n e", n=NT)
    score, kept, rank, weight, rest = (tile8() for _ in range(5))
    gsum, grank = (tile8(E // 2) for _ in range(2))
    won = a.take(NT * E * (E - 1)).rearrange("p (n e d) -> p n e d", n=NT, e=E)
    gwon = a.take(NT * (E // 2) * (E // 2 - 1)).rearrange("p (n e d) -> p n e d", n=NT, e=E // 2)
    exT = a.take(SPAN)
    wsum, winv = a.take(NT), a.take(NT)
    parts = a.take(NT * PARTS * E, BF16).rearrange("p (n k e) -> p n k e", n=NT, k=PARTS)
    wT = a.take(N, BF16)
    silu = a.take(2 * SPAN).rearrange("p (k n) -> p k n", k=2)
    hid = a.take(3 * SPAN).rearrange("p (k n) -> p k n", k=3)
    HID = [0, 1, 2, 0, 1]
    USED = [0, -1, 1, 2, 3]
    yT = a.take(SPAN)
    link_sem = sem(tag + "_vector_chain")
    logits_ready, exT_ready, ex_ready = sem(tag + "_logits"), sem(tag + "_exT"), sem(tag + "_ex")
    parts_ready, wt_ready = sem(tag + "_parts_ready"), sem(tag + "_wt_ready")
    wT_zeroed, wT_ready = sem(tag + "_wT_zeroed"), sem(tag + "_wT_ready")
    gate_ready, up_ready, spread_ready = sem(tag + "_gate"), sem(tag + "_up"), sem(tag + "_spread")
    silu_ready, hid_ready = sem(tag + "_silu"), sem(tag + "_hid")
    prod_ready = sem(tag + "_prod")
    down_done, y_ready = sem(tag + "_down"), sem(tag + "_y")
    yt_ready, x_added = sem(tag + "_yt"), sem(tag + "_x")
    stats_ready, stored = sem(tag + "_stats"), sem(tag + "_stored")
    gate_ps = [b[0][:, 0:SPAN], b[0][:, SPAN:]]
    up_ps = [b[1][:, 0:SPAN], b[1][:, SPAN:]]
    spread_ps = [b[2][:, 0:SPAN], b[2][:, SPAN:]]
    down_ps, back_ps = b[3][:, 0:SPAN], b[3][:, SPAN:]
    logit_ps, ex_ps = b[2][:, 0:SPAN], b[2][:, SPAN:]
    wt_ps = b[3][:, :].bitcast(BF16)

    with nc.Block() as block:
        @block.tensor
        def _(pe):
            def down(i, c, first):
                if c == NCH:
                    pe.wait_ge(prod_ready, i * HCH + HCH)
                else:
                    pe.wait_ge(hid_ready, i * NCH + c + 1)
                if c == 0 and not first:
                    pe.wait_ge(y_ready, i)
                mm = nc.tensor.matmul(down_ps, m.WD[:, c, :], hid[:, HID[c], :], start=(c == 0), stop=(c == NCH))
                if c == NCH:
                    mm.then_inc(down_done, 1)

            def turn_back(n):
                pe.wait_ge(y_ready, n)
                for k in range(TPS):
                    last = nc.tensor.transpose(back_ps[:, k * P:(k + 1) * P], yT[:, k * P:(k + 1) * P], m.ident[:, :])
                last.then_inc(yt_ready, 1)

            def products(i, c, again):
                x = m.xnT[:, bass.ds(i * SPAN, SPAN)]
                if again:
                    pe.wait_ge(silu_ready, i * HCH + USED[c])
                nc.tensor.matmul(gate_ps[c % 2], m.WG[:, c * P:(c + 1) * P], x, start=True, stop=True)\
                    .then_inc(gate_ready, 1)
                if again:
                    pe.wait_ge(prod_ready, i * HCH + USED[c])
                nc.tensor.matmul(up_ps[c % 2], m.WU[:, c * P:(c + 1) * P], x, start=True, stop=True)\
                    .then_inc(up_ready, 1)

            def spread(i, c, again):
                if again:
                    pe.wait_ge(hid_ready, i * NCH + (c - 1))
                nc.tensor.matmul(spread_ps[c % 2], m.sel[:, c * P:(c + 1) * P],
                                 wT[:, bass.ds(i * SPAN, SPAN)], start=True, stop=True)\
                    .then_inc(spread_ready, 1)

            def span(i, first):
                for c in range(HCH):
                    again = not first or c >= 2
                    if again:
                        products(i, c, True)
                    if c < NCH:
                        spread(i, c, again)
                    if c >= 1:
                        down(i, c - 1, first)
                    elif not first:
                        down(i - 1, NCH, False)
                    if c == 1 and not first:
                        turn_back(i)

            for i in range(NSPAN):
                norm_transpose(nc, m, s, pe, i)
            for i in range(NSPAN):
                pe.wait_ge(s.xnT_ready, i + 1)
                last = nc.tensor.matmul(logit_ps[32 * i:32 * (i + 1), :], m.gw[:, :],
                                        m.xnT[:, i * SPAN:(i + 1) * SPAN], start=True, stop=True)
            last.then_inc(logits_ready, 1)
            if tag == "f1":
                pe.wait_ge(m.weights_loaded, 16 * WEIGHT_DMAS)
            products(0, 0, False)
            pe.wait_ge(exT_ready, 1)
            for k in range(TPS):
                last = nc.tensor.transpose(ex_ps[:, k * P:(k + 1) * P], exT[:, k * P:(k + 1) * P], m.ident[:, :])
            last.then_inc(ex_ready, 1)
            products(0, 1, False)
            pe.wait_ge(parts_ready, 1)
            for t in range(NT):
                last = nc.tensor.transpose(wt_ps[0:PARTS * E, t * P:(t + 1) * P],
                                           parts[:, t, :, :].rearrange("p k e -> p (k e)"), m.identb[:, :])
            last.then_inc(wt_ready, 1)
            pe.wait_ge(wT_ready, 1)

            span(0, True)
            with pe.Fori(1, NSPAN) as i:
                span(i, False)
            down(NSPAN - 1, NCH, False)
            turn_back(NSPAN)

        @block.scalar
        def _(act):
            norm_root(nc, m, s, act)
            nc.scalar.activation(m.table[:, :], m.eps[:, :], ACT.Sigmoid)
            for i in range(NSPAN):
                norm_take(nc, m, s, act, i)
            act.wait_ge(logits_ready, 1)
            nc.scalar.activation(exT, logit_ps, ACT.Sigmoid).then_inc(exT_ready, 1)

            def take_out(n):
                act.wait_ge(down_done, n)
                nc.scalar.activation(yT, down_ps, ACT.Copy, scale=0.5).then_inc(y_ready, 1)

            def span(i, first):
                for c in range(HCH):
                    if first and c == 2:
                        act.wait_ge(wT_zeroed, 1)
                        act.wait_ge(wt_ready, 1)
                        nc.scalar.activation(wT[0:PARTS * E, :], wt_ps[0:PARTS * E, :], ACT.Copy)\
                            .then_inc(wT_ready, 1)
                    act.wait_ge(gate_ready, i * HCH + c + 1)
                    if not first or c >= 2:
                        act.wait_ge(prod_ready, i * HCH + USED[c])
                    nc.scalar.activation(silu[:, c % 2, :], gate_ps[c % 2], ACT.Silu).then_inc(silu_ready, 1)
                    if c == 0 and not first:
                        take_out(i)

            span(0, True)
            with act.Fori(1, NSPAN) as i:
                span(i, False)
            take_out(NSPAN)
            if out is None:
                nc.scalar.activation(m.table[:, :], m.eps[:, :], ACT.Sqrt)

        if out is not None:
            @block.sync
            def _(sp):
                out_v = out.rearrange("b (n p) c -> p (b n) c", p=P)
                for i in range(NSPAN):
                    t = slice(i * TPS, (i + 1) * TPS)
                    sp.wait_ge(x_added, i + 1)
                    sp.dma_start(out_v[:, t, :], m.X[:, t, :]).then_inc(stored, 16)
                sp.wait_ge(stored, 16 * NSPAN)

        @block.gpsimd
        def _(pool):
            nc.gpsimd.memset(wT.bitcast(F32), 0.0).then_inc(wT_zeroed, 1)
            if beside is not None:
                pool.wait_ge(wT_zeroed, 1)
                beside(nc, m, sem, pool)

        @block.vector
        def _(dve):
            link = Chain(dve, link_sem)
            norm_vector(nc, m, s, dve)
            dve.wait_ge(ex_ready, 1)
            ex = ex_ps.rearrange("p (k j e) -> p j k e", j=NSPAN, k=TPS)[:, :, :, 0:E]
            for j in range(NSPAN):
                last = nc.vector.tensor_tensor(score[:, j * TPS:(j + 1) * TPS, :], ex[:, j],
                                               m.gb[:, :].unsqueeze(1).to_broadcast([P, TPS, E]), ALU.add)
            link(last)

            def count_better(v, won, rank, n):
                for d in range(1, n):
                    nc.vector.tensor_tensor(won[:, :, d:n, d - 1], v[:, :, 0:n - d], v[:, :, d:n], ALU.is_ge)
                    last = nc.vector.tensor_tensor(won[:, :, 0:d, d - 1], v[:, :, n - d:n], v[:, :, 0:d], ALU.is_gt)
                link(last)
                link(nc.vector.tensor_reduce(rank, won, mybir.AxisListType.X, ALU.add))

            link(nc.vector.tensor_tensor(gsum, score[:, :, 0:E:2], score[:, :, 1:E:2], ALU.add))
            count_better(gsum, gwon, grank, E // 2)
            for k in range(2):
                last = nc.vector.scalar_tensor_tensor(kept[:, :, k:E:2], grank, 2.0, score[:, :, k:E:2],
                                                      ALU.is_lt, ALU.mult)
            link(last)
            count_better(kept, won, rank, E)
            link(nc.vector.scalar_tensor_tensor(weight, rank, 2.0, score, ALU.is_lt, ALU.mult))
            link(nc.vector.tensor_reduce(wsum, weight, mybir.AxisListType.X, ALU.add))
            link(nc.vector.tensor_scalar(wsum, wsum, 1e-20, None, ALU.add))
            link(nc.vector.reciprocal(winv, wsum))
            link(nc.vector.scalar_tensor_tensor(weight, weight, 2.5, winv.unsqueeze(2).to_broadcast([P, NT, E]),
                                                ALU.mult, ALU.mult))
            link(nc.vector.tensor_copy(parts[:, :, 0, :], weight))
            link(nc.vector.tensor_tensor(rest, weight, parts[:, :, 0, :], ALU.subtract))
            link(nc.vector.tensor_copy(parts[:, :, 1, :], rest))
            nc.vector.tensor_tensor(parts[:, :, 2, :], rest, parts[:, :, 1, :], ALU.subtract).then_inc(parts_ready, 1)

            def add_to_x(n):
                dve.wait_ge(yt_ready, n)
                xs = m.X[:, bass.ds((n - 1) * TPS, TPS), :].rearrange("p n c -> p (n c)")
                nc.vector.tensor_tensor(xs, back_ps, xs, ALU.add).then_inc(x_added, 1)
                if out is None:
                    dve.wait_ge(x_added, n)
                    span_stats(nc, m, n - 1, stats_ready)

            def span(i, first):
                for c in range(HCH):
                    dve.wait_ge(silu_ready, i * HCH + c + 1)
                    dve.wait_ge(up_ready, i * HCH + c + 1)
                    h = hid[:, HID[c], :]
                    nc.vector.tensor_tensor(h, silu[:, c % 2, :], up_ps[c % 2], ALU.mult).then_inc(prod_ready, 1)
                    if c < NCH:
                        dve.wait_ge(prod_ready, i * HCH + c + 1)
                        dve.wait_ge(spread_ready, i * NCH + c + 1)
                        nc.vector.tensor_tensor(h, h, spread_ps[c % 2], ALU.mult).then_inc(hid_ready, 1)
                    if c == 2 and not first:
                        add_to_x(i)

            span(0, True)
            with dve.Fori(1, NSPAN) as i:
                span(i, False)
            if out is None:
                for n in range(NSPAN - 1):
                    span_moments(nc, m, dve, n, stats_ready)
            add_to_x(NSPAN)
            if out is None:
                span_moments(nc, m, dve, NSPAN - 1, stats_ready)


def load_quad(nc, m, sp, q_dram, k_dram, q, buf):
    rows = lambda v, lo, hi: v[bass.ds(q * G, G), lo * D:hi * D, :].rearrange("h r t -> r h t")
    for turn in range(PARTS):
        at = turn * PARTS
        sp.dma_start(m.Q[buf][at * D:(at + PARTS) * D, :, :], rows(q_dram, 0, PARTS)).then_inc(m.qk_loaded[buf], 16)
        for lo, hi in ((turn, PARTS), (0, turn)):
            if lo < hi:
                sp.dma_start(m.K[buf][at * D:(at + hi - lo) * D, :, :], rows(k_dram, lo, hi))\
                    .then_inc(m.qk_loaded[buf], 16)
                at += hi - lo


LOAD_DMAS = 3 * PARTS - 1


def project_qkv(nc, m, sem, q_dram, k_dram):
    a = Arena(m)
    banks = [m.psum[i // 2][:, (i % 2) * SPAN:(i % 2 + 1) * SPAN] for i in range(8)]
    s = layer_norm(nc, m, sem, "qkv", a, banks[6:8])
    full, rest = {w: a.take(N) for w in "qk"}, {w: a.take(N) for w in "qk"}
    parts = {w: [a.take(N, BF16) for _ in range(PARTS)] for w in "qk"}
    sign, neg, qbias = a.take(1), a.take(1), a.take(1)
    ksum, kmean = a.take(NSPAN), a.take(B)
    spb = NSPAN // B
    chain, sign_ready, k_done = sem("qkv_chain"), sem("sign_ready"), sem("k_with_bias")
    q_rows, k_rows, v_rows = sem("q_rows"), sem("k_rows"), sem("v_rows")
    v_out = sem("v_out")
    full_ready = {w: sem(w + "_full") for w in "qk"}
    high, middle, rest_ready = ({w: sem(f"{w}_{n}") for w in "qk"} for n in ("high", "middle", "rest"))
    low = {w: sem(w + "_low") for w in "qk"}
    of = lambda v, b: v[:, b * T:(b + 1) * T]
    with nc.Block() as block:
        @block.tensor
        def _(pe):
            def project(w, b, rows, read):
                n = "qk".index(w)
                for i in range(spb * b, spb * (b + 1)):
                    if b:
                        pe.wait_ge(*read)
                    nc.tensor.matmul(banks[2 * n + i % spb], m.WA[:, n * C:(n + 1) * C],
                                     m.xnT[:, i * SPAN:(i + 1) * SPAN], start=True, stop=True).then_inc(rows, 1)

            def values(b):
                for i in range(spb * b, spb * (b + 1)):
                    if b:
                        pe.wait_ge(v_out, i - spb + 1)
                    for k in range(TPS):
                        t = i * TPS + k
                        last = nc.tensor.matmul(banks[4 + i % spb][:, k * P:(k + 1) * P],
                                                m.xnT[:, t * P:(t + 1) * P], m.WA[:, 2 * C:], start=True, stop=True)
                    last.then_inc(v_rows, 1)

            for b in range(B):
                for i in range(spb * b, spb * (b + 1)):
                    norm_transpose(nc, m, s, pe, i)
                if b:
                    values(b - 1)
                pe.wait_ge(s.xnT_ready, spb * (b + 1))
                project("k", b, k_rows, (k_done, spb))
                project("q", b, q_rows, (full_ready["q"], spb))
            values(B - 1)

        @block.scalar
        def _(act):
            norm_root(nc, m, s, act)

            def q_full(b):
                for i in range(spb * b, spb * (b + 1)):
                    act.wait_ge(q_rows, i + 1)
                    nc.scalar.activation(full["q"][:, i * SPAN:(i + 1) * SPAN], banks[i % spb], ACT.Identity,
                                         bias=qbias[:, 0:1], scale=sign[:, 0:1]).then_inc(full_ready["q"], 1)

            def high_part(w, b):
                act.wait_ge(full_ready[w], spb * (b + 1) if w == "q" else b + 1)
                nc.scalar.activation(of(parts[w][0], b), of(full[w], b), ACT.Copy).then_inc(high[w], 1)

            def middle_part(w, b):
                act.wait_ge(rest_ready[w], b + 1)
                nc.scalar.activation(of(parts[w][1], b), of(rest[w], b), ACT.Copy).then_inc(middle[w], 1)

            for i in range(spb):
                norm_take(nc, m, s, act, i)
            act.wait_ge(sign_ready, 1)
            q_full(0)
            high_part("q", 0)
            high_part("k", 0)
            for i in range(spb, NSPAN):
                norm_take(nc, m, s, act, i)
            middle_part("q", 0)
            middle_part("k", 0)
            q_full(1)
            high_part("q", 1)
            high_part("k", 1)
            middle_part("q", 1)
            middle_part("k", 1)

        def rest_part(e, w, b):
            e_wait, op = e
            e_wait(high[w], b + 1)
            op(of(rest[w], b), of(full[w], b), of(parts[w][0], b), ALU.subtract).then_inc(rest_ready[w], 1)

        def low_part(e, w, b):
            e_wait, op = e
            e_wait(middle[w], b + 1)
            op(of(parts[w][2], b), of(rest[w], b), of(parts[w][1], b), ALU.subtract).then_inc(low[w], 1)

        @block.vector
        def _(dve):
            link = Chain(dve, chain)
            link(nc.vector.tensor_scalar(sign, m.gain[:, :], 0.0, None, ALU.is_gt))
            link(nc.vector.tensor_scalar(neg, m.gain[:, :], 0.0, None, ALU.is_lt))
            link(nc.vector.tensor_tensor(sign, sign, neg, ALU.subtract))
            nc.vector.tensor_tensor(qbias, m.bqk[:, 0:1], sign, ALU.mult).then_inc(sign_ready, 1)
            norm_vector(nc, m, s, dve)

            def k_full(b):
                for i in range(spb * b, spb * (b + 1)):
                    dve.wait_ge(k_rows, i + 1)
                    nc.vector.tensor_scalar(full["k"][:, i * SPAN:(i + 1) * SPAN], banks[2 + i % spb], m.bqk[:, 1:2],
                                            0.0, ALU.add, ALU.add, accum_out=ksum[:, i:i + 1]).then_inc(k_done, 1)
                dve.wait_ge(k_done, spb * (b + 1))
                link(nc.vector.tensor_tensor(kmean[:, b:b + 1], ksum[:, spb * b:spb * b + 1],
                                             ksum[:, spb * b + 1:spb * b + 2], ALU.add))
                link(nc.vector.tensor_scalar(kmean[:, b:b + 1], kmean[:, b:b + 1], -1.0 / T, None, ALU.mult))
                nc.vector.tensor_scalar(of(full["k"], b), of(full["k"], b), kmean[:, b:b + 1], None, ALU.add)\
                    .then_inc(full_ready["k"], 1)

            def v_full(b):
                for i in range(spb * b, spb * (b + 1)):
                    dve.wait_ge(v_rows, i + 1)
                    n0 = i * TPS % NB
                    qn = lambda v: v.rearrange("p n (q c) -> p q n c", q=QPB)
                    nc.vector.tensor_tensor(m.V[:, b * QPB:(b + 1) * QPB, n0:n0 + TPS, :],
                                            qn(banks[4 + i % spb].rearrange("p (n c) -> p n c", n=TPS)),
                                            qn(m.bv[:, :].unsqueeze(1).to_broadcast([P, TPS, C])),
                                            ALU.add).then_inc(v_out, 1)

            e = (dve.wait_ge, nc.vector.tensor_tensor)
            k_full(0)
            rest_part(e, "q", 0)
            rest_part(e, "k", 0)
            low_part(e, "q", 0)
            v_full(0)
            low_part(e, "k", 0)
            k_full(1)
            rest_part(e, "k", 1)
            v_full(1)
            low_part(e, "k", 1)

        @block.gpsimd
        def _(pool):
            rest_part((pool.wait_ge, nc.gpsimd.tensor_tensor), "q", 1)
            low_part((pool.wait_ge, nc.gpsimd.tensor_tensor), "q", 1)

        @block.sync
        def _(sp):
            for b in range(B):
                for n, ready in enumerate((high, middle, low)):
                    for w, dram in (("q", q_dram), ("k", k_dram)):
                        sp.wait_ge(ready[w], b + 1)
                        rows = dram[b * N_HEAD:(b + 1) * N_HEAD, n * D:(n + 1) * D, :]
                        sp.dma_start(rows, of(parts[w][n], b)).then_inc(m.parts_stored[b], 16)
                if b == 0:
                    sp.wait_ge(m.parts_stored[0], 16 * 2 * PARTS)
                    load_quad(nc, m, sp, q_dram, k_dram, 0, 0)


def attention(nc, m, sem, q_dram, k_dram, att_dram):
    a = Arena(m)
    Q, K, masks, Vq = m.Q, m.K, m.masks, m.Vq
    wide_tile = lambda: a.take(G * T).rearrange("p (g t) -> p g t", g=G)
    half_tile = lambda: a.take(G * SPAN).rearrange("p (g t) -> p g t", g=G)
    relus, powers = [wide_tile() for _ in range(2)], [wide_tile() for _ in range(NR - 1)] + [half_tile()]
    relus = [relus[0], relus[1], relus[0], relus[1], half_tile()]
    Y = lambda r, g: relus[r][:, g, :]
    Z = lambda r, g: powers[r][:, g, :]
    off = lambda r: SPAN if r == NR - 1 else 0
    sums = a.take(T)
    tiles = m.psum[0:3]
    acc = m.psum[3]

    lower_ready, upper_ready = sem("lower_ready"), sem("upper_ready")
    relu_done, square_done = sem("relu_done"), sem("square_done")
    upper_v, upper_a = sem("upper_summed_vector"), sem("upper_summed_scalar")
    fourth_p, fourth_a = sem("fourth_gpsimd"), sem("fourth_scalar")
    sums_out, sums_stored = sem("sums_out"), sem("sums_stored")
    power_summed, relu_summed = sem("power_round_summed"), sem("relu_round_summed")
    sums_free = sem("sums_free")
    vq_ready, num_loaded = sem("vq_ready"), m.num_loaded
    steps = [(r, g) for r in range(NR) for g in range(G)]
    count = lambda who, upto, inclusive=True: sum(who(r, g) for r, g in steps[:steps.index(upto) + inclusive])
    all_of = lambda who: sum(who(r, g) for r, g in steps)
    by_v, by_a = upper_by_vector, lambda r, g: not upper_by_vector(r, g)
    sq_p, sq_a = square_by_gpsimd, lambda r, g: not square_by_gpsimd(r, g)
    NV, NA, NP4, NA4 = all_of(by_v), all_of(by_a), all_of(sq_p), all_of(sq_a)
    order = []
    for r, g in steps:
        order += [("both", r, g)] if r == NR - 1 else [("lower", r, g), ("upper", r, g)]
    assert len(order) % 3 == 0
    slot = {}
    for n, (kind, r, g) in enumerate(order):
        for k in ("lower", "upper") if kind == "both" else (kind,):
            slot[k, r, g] = n % 3

    def quads(engine, body):
        body(0, 0, 1)
        with engine.Fori(0, NQUAD // 2 - 1) as pair:
            body(2 * pair + 1, 1, pair + 1)
            body(2 * pair + 2, 0, pair + 2)
        body(NQUAD - 1, 1, NQUAD // 2)

    first_quad = lambda q: isinstance(q, int) and q == 0
    last_quad = lambda q: isinstance(q, int) and q == NQUAD - 1

    with nc.Block() as block:
        @block.sync
        def _(sp):
            def store(n):
                sp.wait_ge(sums_out, n)
                for g in range(G):
                    head = att_dram[bass.ds((n - 1) * G + g, 1)].rearrange("h k d t -> (h k d) t")
                    sp.dma_start(head, sums[32 * g:32 * (g + 1), :]).then_inc(sums_stored, 16)
                sp.wait_ge(sums_stored, 16 * G * n)
                sp.sem_inc(sums_free, 1)

            def body(q, buf, nth):
                if not last_quad(q):
                    if not first_quad(q):
                        sp.wait_ge(upper_ready, q * STEPS)
                    load_quad(nc, m, sp, q_dram, k_dram, q + 1, 1 - buf)
                if not first_quad(q):
                    store(q)

            sp.sem_inc(sums_free, 1)
            sp.wait_ge(m.parts_stored[1], 16 * 2 * PARTS)
            quads(sp, body)
            sp.dma_start(m.xnT[:, 0:T], att_dram[0:N_HEAD, 0, :, :]).then_inc(num_loaded, 16)
            sp.dma_start(m.xnT[0:P - G * D, T:], att_dram[N_HEAD:B * N_HEAD - G, 0, :, :]).then_inc(num_loaded, 16)
            store(NQUAD)

        @block.tensor
        def _(pe):
            def wait_tile(q, r, g, kind):
                n = next(i for i, (k, rr, gg) in enumerate(order) if (rr, gg) == (r, g) and k in (kind, "both"))
                back = n - 3
                if back < 0 and first_quad(q):
                    return
                k, rr, gg = order[back]
                qq = q - 1 if back < 0 else q
                at = (rr, gg)
                if k in ("lower", "both"):
                    pe.wait_ge(relu_done, qq * STEPS + steps.index(at) + 1)
                if k in ("upper", "both"):
                    if by_v(*at):
                        pe.wait_ge(upper_v, qq * NV + count(by_v, at))
                    else:
                        pe.wait_ge(upper_a, qq * NA + count(by_a, at))

            def fill(q, par, r, g, kind):
                left, right = (K, Q) if kind == "lower" else (Q, K)
                bank = tiles[slot[kind, r, g]]
                shift = -SPAN if (r == NR - 1 and kind == "upper") else 0
                for blk, col, seq in tile_blocks(r):
                    for lo, hi in bank_pieces(col, col + width(blk)):
                        s0 = seq + lo - col
                        last = nc.tensor.matmul(bank[:, lo + shift:hi + shift], left[par][:, g, blk * P:(blk + 1) * P],
                                                right[par][:, g, s0:s0 + hi - lo], start=True, stop=True)
                last.then_inc(lower_ready if kind == "lower" else upper_ready, 1)

            def pieces(q, what, r):
                skip = P if what == "relu" else 0
                cut = [(blk, lo, hi, seq - col) for blk, col, seq in tile_blocks(r)
                       for lo, hi in bank_pieces(col + skip, col + width(blk))]
                return [(q, what, r, n == 0, n == len(cut) - 1, *c) for n, c in enumerate(cut)]

            def add_piece(q, what, r, first, last, blk, lo, hi, to_seq):
                if first and what == "relu":
                    pe.wait_ge(relu_done, q * STEPS + (r + 1) * G)
                    if r == 0 and not first_quad(q):
                        pe.wait_ge(sums_out, q)
                if first and what == "power":
                    pe.wait_ge(fourth_p, q * NP4 + count(sq_p, (r, G - 1)))
                    pe.wait_ge(fourth_a, q * NA4 + count(sq_a, (r, G - 1)))
                    if r == 0:
                        pe.wait_ge(vq_ready, q + 1)
                s0 = lo + to_seq
                start = what == "relu" and r == 0
                stop = what == "power" and (r == NR - 1 or (r == NR - 2 and s0 < SPAN))
                for g in range(G):
                    src = (Z if what == "power" else Y)(r, g)[:, lo - off(r):hi - off(r)]
                    w = Vq[:, blk, g, :] if what == "power" else m.ones_rows[:, :]
                    mm = nc.tensor.matmul(acc[32 * g:32 * (g + 1), s0:s0 + hi - lo], w, src, start=start,
                                          stop=stop, skip_group_check=True)
                if last:
                    mm.then_inc(relu_summed if what == "relu" else power_summed, 1)

            def plan(q, r):
                last = [] if first_quad(q) else [q - 1]
                some = lambda quad, what, rr: [x for p in quad for x in pieces(p, what, rr)]
                if r == 1:
                    return [some(last, "power", 4), [], some([q], "relu", 0), []]
                work = {0: some(last, "relu", 3) + some(last, "power", 3) + some(last, "relu", 4),
                        2: some([q], "power", 0) + some([q], "relu", 1),
                        3: some([q], "power", 1) + some([q], "relu", 2),
                        4: some([q], "power", 2)}[r]
                return [work[g * len(work) // G:(g + 1) * len(work) // G] for g in range(G)]

            def body(q, buf, nth):
                pe.wait_ge(m.qk_loaded[buf], nth * (16 * LOAD_DMAS))
                for r, g in steps:
                    for kind in ("lower", "upper"):
                        if kind == "lower" or r < NR - 1:
                            wait_tile(q, r, g, kind)
                        fill(q, buf, r, g, kind)
                    for piece in plan(q, r)[g]:
                        add_piece(*piece)

            quads(pe, body)
            for what, r in (("relu", 3), ("power", 3), ("relu", 4), ("power", 4)):
                for piece in pieces(NQUAD - 1, what, r):
                    add_piece(*piece)

        @block.vector
        def _(dve):
            def body(q, buf, nth):
                for r, g in steps:
                    lo, hi = tile_low(r), T
                    before = {0: -3, 1: -2, 2: 0, 3: 1, 4: -1}[r]
                    if r in (2, 3) or not first_quad(q):
                        dve.wait_ge(relu_summed, q * NR + before + 1)
                        dve.wait_ge(square_done, (q * NR + before) * G + g + 1)
                    dve.wait_ge(lower_ready, q * STEPS + r * G + g + 1)
                    mask = masks[:, 0, 0:SPAN] if r == NR - 1 else masks[:, r, lo:hi]
                    nc.vector.scalar_tensor_tensor(Y(r, g)[:, lo - off(r):hi - off(r)],
                                                   tiles[slot["lower", r, g]][:, lo:hi], 0.0, mask,
                                                   ALU.max, ALU.mult).then_inc(relu_done, 1)
                    if by_v(r, g):
                        dve.wait_ge(upper_ready, q * STEPS + r * G + g + 1)
                        shift = -SPAN if r == NR - 1 else 0
                        for blk, col, seq in tile_blocks(r):
                            src = tiles[slot["upper", r, g]][:, col + shift:col + width(blk) + shift]
                            last = nc.vector.tensor_scalar(src, src, 0.0, 0.0, ALU.max, ALU.add,
                                                           accum_out=m.upper[:, blk, bass.ds(q * G + g, 1)])
                        last.then_inc(upper_v, 1)
            quads(dve, body)

        @block.scalar
        def _(act):
            def evacuate(n):
                act.wait_ge(power_summed, n * NR)
                act.wait_ge(sums_free, n)
                nc.scalar.activation(sums, acc[:, :], ACT.Copy).then_inc(sums_out, 1)

            def body(q, buf, nth):
                for r, g in steps:
                    if (r, g) == (1, 1) and not first_quad(q):
                        evacuate(q)
                    n = q * STEPS + r * G + g + 1
                    if by_a(r, g):
                        act.wait_ge(upper_ready, n)
                        shift = -SPAN if r == NR - 1 else 0
                        for blk, col, seq in tile_blocks(r):
                            src = tiles[slot["upper", r, g]][:, col + shift:col + width(blk) + shift]
                            last = nc.scalar.activation(src, src, ACT.Relu,
                                                        accum_out=m.upper[:, blk, bass.ds(q * G + g, 1)])
                        last.then_inc(upper_a, 1)
                    lo = tile_low(r) - off(r)
                    hi = T - off(r)
                    z = Z(r, g)[:, lo:hi]
                    if not first_quad(q):
                        act.wait_ge(power_summed, (q - 1) * NR + r + 1)
                    elif (r, g) == (0, 0):
                        act.wait_ge(m.parts_stored[1], 16 * 2 * PARTS)
                    act.wait_ge(relu_done, n)
                    nc.scalar.activation(z, Y(r, g)[:, lo:hi], ACT.Square).then_inc(square_done, 1)
                    if sq_a(r, g):
                        act.wait_ge(square_done, n)
                        nc.scalar.activation(z, z, ACT.Square).then_inc(fourth_a, 1)
            quads(act, body)
            evacuate(NQUAD)

        @block.gpsimd
        def _(pool):
            def copy_v(q):
                src = m.V[:, bass.ds(q, 1), :, :].rearrange("p q n (g d) -> p (q n) g d", g=G)
                nc.gpsimd.tensor_copy(Vq[:, :, :, 0:D], src).then_inc(vq_ready, 1)

            def body(q, buf, nth):
                for r, g in steps:
                    if (r, g) == (1, 0) and not first_quad(q):
                        pool.wait_ge(power_summed, q * NR)
                        copy_v(q)
                    if sq_p(r, g):
                        pool.wait_ge(square_done, q * STEPS + r * G + g + 1)
                        lo = tile_low(r) - off(r)
                        hi = T - off(r)
                        z = Z(r, g)[:, lo:hi]
                        nc.gpsimd.tensor_tensor(z, z, z, ALU.mult).then_inc(fourth_p, 1)
            copy_v(0)
            nc.gpsimd.tensor_tensor(m.X[:, :, :], m.X[:, :, :], m.bp[:, :].unsqueeze(1).to_broadcast([P, NT, C]),
                                    ALU.add)
            quads(pool, body)


def merge_heads(nc, m, sem, att_dram):
    a = Arena(m)
    HEADS = B * N_HEAD
    QT = T // QUARTERS
    num = m.xnT
    den, low, mad, rden = a.take(QT), a.take(QT), a.take(QT), a.take(QT)
    att = a.take(N)
    ginv = a.take(1)
    loaded, chain = sem("merge_loaded"), sem("merge_chain")
    upper_t, rden_ready, spread_ready = sem("upper_t"), sem("rden_ready"), sem("rden_spread")
    att_ready, proj_ready = sem("att_ready"), sem("proj_ready")
    x_added, stats_ready = sem("attention_added"), sem("attention_stats")
    upper_ps = m.psum[0][:, 0:QT]
    spread_ps = m.psum[1:3]
    proj_ps = [m.psum[3][:, 0:SPAN], m.psum[3][:, SPAN:], m.psum[0][:, 0:SPAN], m.psum[0][:, SPAN:]]
    with nc.Block() as block:
        @block.sync
        def _(sp):
            for n in range(QUARTERS):
                for k, dst in ((2, low), (1, den)):
                    sp.dma_start(dst[n * HEADS:(n + 1) * HEADS, :], att_dram[:, k, 0, n * QT:(n + 1) * QT])\
                        .then_inc(loaded, 16)
            sp.dma_start(num[P - G * D:, T:], att_dram[HEADS - G:, 0, :, :]).then_inc(m.num_loaded, 16)

        @block.tensor
        def _(pe):
            per = NB // QUARTERS
            for i in range(NB):
                n, k = i // per, i % per
                last = nc.tensor.matmul(upper_ps[n * HEADS:(n + 1) * HEADS, k * P:(k + 1) * P], m.upper[:, i, :],
                                        m.ident[:, :], start=True, stop=True)
            last.then_inc(upper_t, 1)
            pe.wait_ge(rden_ready, 1)
            for b in range(B):
                for n in range(QUARTERS):
                    last = nc.tensor.matmul(spread_ps[b][:, n * QT:(n + 1) * QT], m.spread[:, n, b, :], rden,
                                            start=True, stop=True)
                    if n % (QUARTERS // 2) == QUARTERS // 2 - 1:
                        last.then_inc(spread_ready, 1)
            for i in range(NSPAN):
                pe.wait_ge(att_ready, i + 1)
                for k in range(TPS):
                    t = i * TPS + k
                    last = nc.tensor.matmul(proj_ps[i][:, k * P:(k + 1) * P], att[:, t * P:(t + 1) * P],
                                            m.WP[:, :], start=True, stop=True)
                last.then_inc(proj_ready, 1)

        @block.scalar
        def _(act):
            nc.scalar.activation(m.table[:, :], m.eps[:, :], ACT.Sqrt)

        @block.vector
        def _(dve):
            link = Chain(dve, chain)
            link(nc.vector.reciprocal(ginv, m.gain[:, :]))
            dve.wait_ge(upper_t, 1)
            dve.wait_ge(loaded, 16 * 2 * QUARTERS)
            link(nc.vector.tensor_tensor(mad, upper_ps, low, ALU.add))
            link(nc.vector.tensor_scalar(mad, mad, 2.0 / T, 1e-6, ALU.mult, ALU.add))
            link(nc.vector.tensor_scalar(mad, mad, ginv[:, 0:1], None, ALU.mult))
            link(nc.vector.tensor_tensor(mad, mad, mad, ALU.mult))
            link(nc.vector.tensor_tensor(mad, mad, mad, ALU.mult))
            link(nc.vector.scalar_tensor_tensor(rden, mad, 1e-6, den, ALU.mult, ALU.add))
            nc.vector.reciprocal(rden, rden).then_inc(rden_ready, 1)
            dve.wait_ge(m.num_loaded, 16 * 3)
            for i in range(NSPAN):
                dve.wait_ge(spread_ready, i + 1)
                sl = slice(i * SPAN, (i + 1) * SPAN)
                rd = spread_ps[i // 2][:, (i % 2) * SPAN:(i % 2 + 1) * SPAN]
                nc.vector.tensor_tensor(att[:, sl], num[:, sl], rd, ALU.mult).then_inc(att_ready, 1)
            for i in range(NSPAN):
                dve.wait_ge(proj_ready, i + 1)
                xs = m.X[:, i * TPS:(i + 1) * TPS, :].rearrange("p n c -> p (n c)")
                nc.vector.tensor_tensor(xs, proj_ps[i], xs, ALU.add).then_inc(x_added, 1)
                dve.wait_ge(x_added, i + 1)
                span_stats(nc, m, i, stats_ready)
                span_moments(nc, m, dve, i, stats_ready)


_INS = ['L0_attn_x', 'L0_attn_W_attn', 'L0_attn_b_attn', 'L0_attn_W_proj', 'L0_attn_b_proj', 'L0_attn_score_gain',
        'L0_ffn_gate_w', 'L0_ffn_gate_bias', 'L0_ffn_w_gate', 'L0_ffn_w_up', 'L0_ffn_w_down', 'L0_ffn_sw_gate',
        'L0_ffn_sw_up', 'L0_ffn_sw_down']


def kernel(**inputs):
    import numpy as np
    import concourse.bacc as bacc
    from concourse.bass_utils import run_bass_kernel_spmd

    nc = bacc.Bacc("TRN2", target_bir_lowering=False, num_devices=1)
    arrays, args = {}, []
    for name in _INS:
        a = np.ascontiguousarray(inputs[name])
        if a.ndim == 0:
            a = a.reshape(1, 1)
        arrays[f"in_{name}"] = a
        args.append(nc.dram_tensor(f"in_{name}", a.shape, mybir.dt.from_np(a.dtype), kind="ExternalInput").ap())
    out = nc.dram_tensor("out_x", (B, T, C), F32, kind="ExternalOutput").ap()
    build(nc, *args, out)
    r = run_bass_kernel_spmd(nc, [arrays], core_ids=[0])
    return r.results[0]["out_x"]
```

```python
from contextlib import ExitStack

import concourse.bass as bass
from concourse import mybir

F32 = mybir.dt.float32
BF16 = mybir.dt.bfloat16
ALU = mybir.AluOpType
ACT = mybir.ActivationFunctionType

P = 128
B, T, C = 2, 1024, 128
N_HEAD = 16
D = C // N_HEAD
N = B * T
NT = N // P
SPAN = 512
NSPAN = N // SPAN
TPS = SPAN // P
E, I = 8, 64
NCH = E * I // P
HCH = NCH + 1
EPS = 1e-5

PARTS = 3
G = 4
NQUAD = B * N_HEAD // G
QPB = NQUAD // B
NB = T // P
ROUNDS = [(0, None), (1, 7), (2, 6), (3, 5), (4, None)]
NR = len(ROUNDS)
STEPS = NR * G
HB = B * N_HEAD
QUARTERS = P // HB
QT = T // QUARTERS
HEAD_ROW = [N_HEAD, 0]


def width(block):
    return T - block * P


def tile_blocks(r):
    main, extra = ROUNDS[r]
    out = [(main, main * P, main * P)]
    if extra is not None:
        out.append((extra, 0, extra * P))
    return out


def tile_low(r):
    main, extra = ROUNDS[r]
    return 0 if extra is not None else main * P


def bank_pieces(lo, hi):
    return [(a, b) for a, b in ((lo, min(hi, SPAN)), (max(lo, SPAN), hi)) if a < b]


def upper_by_vector(r, g):
    return g % 2 == 1


def square_by_gpsimd(r, g):
    return g < 3


class Chain:

    def __init__(self, engine, sem):
        self.engine, self.sem, self.n = engine, sem, 0

    def __call__(self, instruction):
        self.n += 1
        instruction.then_inc(self.sem, 1)
        self.engine.wait_ge(self.sem, self.n)


def build(nc, x_in, w_attn, b_attn, w_proj, b_proj, score_gain, gate_w, gate_bias,
          w_gate, w_up, w_down, sw_gate, sw_up, sw_down, out):
    ctx = ExitStack()
    with ctx:
        def sb(name, shape, dt=F32):
            return ctx.enter_context(nc.sbuf_tensor(name, shape, dt))

        def sem(name):
            return ctx.enter_context(nc.semaphore(name))

        m = type("Memory", (), {})()
        m.X = sb("X", [P, NT, C])
        m.xnT = sb("xnT", [P, N])
        m.WG = sb("WG", [P, HCH * P])
        m.WU = sb("WU", [P, HCH * P])
        m.WD = sb("WD", [P, HCH, C])
        m.WA = sb("WA", [P, 3 * C])
        m.WP = sb("WP", [P, C])
        m.gw = sb("gw", [P, 32])
        m.gb = sb("gb", [P, E])
        m.bqk = sb("bqk", [P, 2])
        m.bv = sb("bv", [P, C])
        m.bp = sb("bp", [P, C])
        m.gain = sb("gain", [P, 1])
        m.slope = sb("slope", [P, 1])
        m.ident = sb("ident", [P, P])
        m.identb = sb("identb", [P, P], BF16)
        m.sel = sb("sel", [P, NCH * P], BF16)
        m.ones_rows = sb("ones_rows", [P, 32])
        m.V = sb("V", [P, NQUAD, NB, G * D])
        m.upper = sb("upper", [P, NB, (B + 2) * N_HEAD])
        m.den = [sb(f"den{i}", [P, QT]) for i in range(B)]
        m.low = [sb(f"low{i}", [P, QT]) for i in range(B)]
        m.stats = sb("stats", [P, NT, 6])
        m.mv = sb("mv", [P, NT, 2])
        m.eps = sb("eps", [P, 1])
        m.table = sb("table", [P, 1])
        m.spread = sb("spread", [P, QUARTERS, B, N_HEAD * D])
        m.pick = sb("pick", [P, 2, HB])
        m.Q = [sb(f"Q{i}", [P, G, T], BF16) for i in range(2)]
        m.K = [sb(f"K{i}", [P, G, T], BF16) for i in range(2)]
        m.masks = sb("masks", [P, NR - 1, T], BF16)
        m.Vq = sb("Vq", [P, NB, G, 32])
        m.arena = sb("arena", [P, 29 * 1024])
        m.psum = [ctx.enter_context(nc.psum_tensor(f"bank{i}", [P, 2 * SPAN], F32)) for i in range(4)]

        q_dram = nc.dram_tensor("q_parts", [B * N_HEAD, PARTS * D, T], BF16, kind="Internal").ap()
        k_dram = nc.dram_tensor("k_parts", [B * N_HEAD, PARTS * D, T], BF16, kind="Internal").ap()
        att_dram = nc.dram_tensor("att", [B * N_HEAD, 4, D, T], F32, kind="Internal").ap()

        m.gate_loaded = sem("gate_loaded")
        m.ffn_loaded, m.attention_loaded = sem("ffn_weights_loaded"), sem("attention_weights_loaded")
        m.parts_stored = sem("parts_stored")
        m.qk_loaded = [sem("qk_loaded0"), sem("qk_loaded1")]
        load_x(nc, m, sem, x_in, gate_w, gate_bias)
        qkv_norm = layer_norm(nc, m, sem, "qkv", Arena(m, NORM_AT), [m.psum[2][:, 0:SPAN], m.psum[2][:, SPAN:]], B)
        weights = (w_attn, b_attn, w_proj, b_proj, score_gain, w_gate, w_up, w_down, sw_gate, sw_up, sw_down)
        ffn(nc, m, sem, "f1", attention_constants, lambda sp: load_weights(m, sp, *weights), qkv_norm)
        store_rest = project_qkv(nc, m, sem, qkv_norm, q_dram, k_dram)
        f2_norm = layer_norm(nc, m, sem, "f2", Arena(m, NORM_AT),
                             [m.psum[2][:, 0:SPAN], m.psum[2][:, SPAN:], m.psum[0][:, 0:SPAN], m.psum[1][:, 0:SPAN]], B)
        attention(nc, m, sem, q_dram, k_dram, att_dram, store_rest, f2_norm)
        ffn(nc, m, sem, "f2", out=out, s=f2_norm)


NORM_AT = 12 * 1024


class Arena:

    def __init__(self, m, at=0):
        self.flat, self.at = m.arena, at

    def take(self, n, dt=F32):
        words = n if dt == F32 else n // 2
        view = self.flat[:, self.at:self.at + words]
        self.at += words
        assert self.at <= self.flat.shape[1], self.at
        return view if dt == F32 else view.bitcast(dt)


FFN_DMAS, ATTENTION_DMAS = 6, 7


def load_weights(m, sp, w_attn, b_attn, w_proj, b_proj, score_gain, w_gate, w_up, w_down, sw_gate, sw_up, sw_down):
    row = lambda v: v.rearrange("(a n) -> a n", a=1)
    by_h = lambda v: v.rearrange("h (e i) -> h e i", e=E)
    for dst, src in ((by_h(m.WG[:, 0:E * I]), w_gate.rearrange("e h i -> h e i")),
                     (by_h(m.WU[:, 0:E * I]), w_up.rearrange("e h i -> h e i")),
                     (m.WD[:, 0:NCH, :], w_down.rearrange("(c e) i h -> (e i) c h", e=E // NCH)),
                     (m.WG[:, E * I:], sw_gate), (m.WU[:, E * I:], sw_up), (m.WD[:, NCH, :], sw_down)):
        sp.dma_start(dst, src).then_inc(m.ffn_loaded, 16)
    for dst, src in ((m.WA[:, :], w_attn), (m.WP[:, :], w_proj),
                     (m.bqk[:, 0:1], b_attn[0:C].rearrange("(p a) -> p a", a=1)),
                     (m.bqk[:, 1:2], b_attn[C:2 * C].rearrange("(p a) -> p a", a=1)),
                     (m.bv[:, :], row(b_attn[2 * C:3 * C]).to_broadcast([P, C])),
                     (m.bp[:, :], row(b_proj).to_broadcast([P, C])),
                     (m.gain[:, :], score_gain.to_broadcast([P, 1]))):
        sp.dma_start(dst, src).then_inc(m.attention_loaded, 16)
    sp.wait_ge(m.attention_loaded, 16 * ATTENTION_DMAS)


def load_x(nc, m, sem, x_in, gate_w, gate_bias):
    x_loaded, made = [sem(f"x_loaded{i}") for i in range(NSPAN)], sem("constants_made")
    gw_zeroed, stats_ready = sem("gw_zeroed"), sem("x_stats")
    x_v = x_in.rearrange("b (n p) c -> p (b n) c", p=P)
    with nc.Block() as block:
        @block.sync
        def _(sp):
            for i in range(NSPAN):
                t = slice(i * TPS, (i + 1) * TPS)
                sp.dma_start(m.X[:, t, :], x_v[:, t, :]).then_inc(x_loaded[i], 16)

        @block.scalar
        def _(act):
            act.wait_ge(gw_zeroed, 1)
            act.dma_start(m.gw[:, 0:E], gate_w).then_inc(m.gate_loaded, 16)
            act.dma_start(m.gb[:, :], gate_bias.rearrange("(a n) -> a n", a=1).to_broadcast([P, E]))\
                .then_inc(m.gate_loaded, 16)
            act.wait_ge(made, 1)
            nc.scalar.activation(m.table[:, :], m.eps[:, :], ACT.Sqrt)

        @block.gpsimd
        def _(pool):
            nc.gpsimd.memset(m.gw[:, :], 0.0).then_inc(gw_zeroed, 1)
            nc.gpsimd.memset(m.eps[:, :], EPS).then_inc(made, 1)
            nc.gpsimd.memset(m.ident[:, :], 0.0).then_inc(made, 1)
            nc.gpsimd.memset(m.identb[:, :], 0.0).then_inc(made, 1)
            nc.gpsimd.memset(m.sel[:, :], 0.0).then_inc(made, 1)
            link = Chain(pool, made)
            link.n = 4
            for t in (m.ident, m.identb):
                pool.wait_ge(made, 4)
                link(nc.gpsimd.affine_select(out=t[:, :], in_=t[:, :], compare_op=ALU.not_equal, fill=1.0,
                                             base=0, pattern=[[-1, P]], channel_multiplier=1))
            for part in range(PARTS):
                link(nc.gpsimd.affine_select(out=m.sel[:, :], in_=m.sel[:, :], compare_op=ALU.not_equal,
                                             fill=1.0, base=-E * part, pattern=[[-1, E], [0, I]],
                                             channel_multiplier=1))

        @block.vector
        def _(dve):
            for i in range(NSPAN):
                dve.wait_ge(x_loaded[i], 16)
                span_stats(nc, m, i, stats_ready)
                span_moments(nc, m, dve, i, stats_ready)


def attention_constants(nc, m, sem, pool):
    zeroed, made = sem("operands_zeroed"), sem("attention_constants")
    for t in (*m.Q, *m.K):
        nc.gpsimd.memset(t[64:P, :, :].rearrange("p g t -> p (g t)").bitcast(F32), 0.0).then_inc(zeroed, 1)
    pool.wait_ge(zeroed, 4)
    nc.gpsimd.memset(m.ones_rows[:, :], 0.0).then_inc(made, 1)
    nc.gpsimd.memset(m.spread[:, :, :, :], 0.0).then_inc(made, 1)
    nc.gpsimd.memset(m.Vq[:, :, :, :], 0.0).then_inc(made, 1)
    nc.gpsimd.memset(m.masks[:, :, :], 1.0).then_inc(made, 1)
    nc.gpsimd.memset(m.pick[:, :, :], 0.0)
    nc.gpsimd.memset(m.upper[:, :, :], 0.0)
    for b in range(B):
        nc.gpsimd.memset(m.den[b][:, :], 1.0)
        nc.gpsimd.memset(m.low[b][:, :], 0.0)
    link = Chain(pool, made)
    link.n = 4
    pool.wait_ge(made, 4)
    link(nc.gpsimd.memset(m.ones_rows[:, 2 * D:3 * D], 1.0))
    link(nc.gpsimd.memset(m.Vq[:, :, :, D:2 * D], 1.0))
    for n in range(QUARTERS):
        last = nc.gpsimd.affine_select(out=m.spread[:, n], in_=m.spread[:, n], compare_op=ALU.not_equal,
                                       fill=1.0, base=-HB * n - HEAD_ROW[0],
                                       pattern=[[HEAD_ROW[0] - HEAD_ROW[1], B], [-1, N_HEAD], [0, D]],
                                       channel_multiplier=1)
    nc.gpsimd.affine_select(out=m.pick[:, :, :], in_=m.pick[:, :, :], compare_op=ALU.not_equal, fill=1.0,
                            base=32 * (HEAD_ROW[B - 1] + N_HEAD - G) - D, pattern=[[-D, 2], [-32, HB]],
                            channel_multiplier=1)
    for r in range(NR - 1):
        for blk, col, seq in tile_blocks(r):
            d = m.masks[:, r, col:col + P]
            last = nc.gpsimd.affine_select(out=d, in_=d, compare_op=ALU.is_ge, fill=0.0, base=0,
                                           pattern=[[1, P]], channel_multiplier=-1)
    link(last)
    for n in range(QUARTERS):
        link(nc.gpsimd.memset(m.den[B - 1][n * HB:n * HB + N_HEAD, :], 0.0))


def span_stats(nc, m, i, stats_ready):
    for k in range(TPS):
        t = bass.ds(i * TPS + k, 1)
        last = nc.vector.bn_stats(m.stats[:, t, :].rearrange("p a k -> p (a k)"),
                                  m.X[:, t, :].rearrange("p a c -> p (a c)"))
    last.then_inc(stats_ready, 1)


def span_moments(nc, m, dve, i, stats_ready):
    dve.wait_ge(stats_ready, i + 1)
    for t in range(i * TPS, (i + 1) * TPS):
        last = nc.vector.bn_aggr(m.mv[:, t, :], m.stats[:, t, :])
    return last


def layer_norm(nc, m, sem, tag, a, banks, parts=1):
    s = type("Norm", (), {})()
    s.xn = a.take(NT * C).rearrange("p (n c) -> p n c", n=NT)
    s.std = a.take(NT)
    s.rstd = a.take(NT)
    s.shift = a.take(NT)
    s.xn_ready_a = sem(tag + "_xn_ready_scalar")
    s.banks = banks
    s.parts = [slice(i * NT // parts, (i + 1) * NT // parts) for i in range(parts)]
    s.moments_ready = sem(tag + "_moments")
    s.std_ready, s.rstd_ready = sem(tag + "_std_ready"), sem(tag + "_rstd_ready")
    s.xn_ready, s.xt_ready, s.xnT_ready = sem(tag + "_xn_ready"), sem(tag + "_xt_ready"), sem(tag + "_xnT_ready")
    return s


def norm_vector(nc, m, s, dve, part=0):
    t = s.parts[part]
    dve.wait_ge(s.std_ready, part + 1)
    nc.vector.reciprocal(s.rstd[:, t], s.std[:, t]).then_inc(s.rstd_ready, 1)
    dve.wait_ge(s.rstd_ready, 2 * part + 1)
    nc.vector.scalar_tensor_tensor(s.shift[:, t], m.mv[:, t, 0], -1.0, s.rstd[:, t], ALU.mult, ALU.mult)\
        .then_inc(s.rstd_ready, 1)
    for t in range(t.start, t.stop):
        if t % TPS < TPS - 1:
            nc.vector.tensor_scalar(s.xn[:, t, :], m.X[:, t, :], m.mv[:, t, 0:1], s.rstd[:, t:t + 1],
                                    ALU.subtract, ALU.mult).then_inc(s.xn_ready, 1)


def norm_root(nc, m, s, act, part=0):
    t = s.parts[part]
    nc.scalar.activation(s.std[:, t], m.mv[:, t, 1], ACT.Sqrt, bias=m.eps[:, 0:1]).then_inc(s.std_ready, 1)


def norm_last_tile(nc, m, s, act, i):
    t = (i + 1) * TPS - 1
    part = [t < p.stop for p in s.parts].index(True)
    act.wait_ge(s.rstd_ready, 2 * part + 2)
    nc.scalar.activation(s.xn[:, t, :], m.X[:, t, :], ACT.Identity, bias=s.shift[:, t:t + 1],
                         scale=s.rstd[:, t:t + 1]).then_inc(s.xn_ready_a, 1)


def norm_take(nc, m, s, act, i):
    act.wait_ge(s.xt_ready, i + 1)
    nc.scalar.activation(m.xnT[:, i * SPAN:(i + 1) * SPAN], s.banks[i % len(s.banks)], ACT.Copy)\
        .then_inc(s.xnT_ready, 1)


def norm_transpose(nc, m, s, pe, i):
    if i >= 2:
        pe.wait_ge(s.xnT_ready, i - 1)
    for k in range(TPS):
        t = i * TPS + k
        if k < TPS - 1:
            pe.wait_ge(s.xn_ready, i * (TPS - 1) + k + 1)
        else:
            pe.wait_ge(s.xn_ready_a, i + 1)
        last = nc.tensor.transpose(s.banks[i % len(s.banks)][:, k * P:(k + 1) * P], s.xn[:, t, :], m.ident[:, :])
    last.then_inc(s.xt_ready, 1)


def ffn(nc, m, sem, tag, beside=None, load=None, following=None, out=None, s=None):
    a = Arena(m)
    b = m.psum
    normed = NSPAN // B if s is not None else 0
    s = s or layer_norm(nc, m, sem, tag, a, [b[0][:, 0:SPAN], b[1][:, 0:SPAN]])
    part = len(s.parts) - 1
    tile8 = lambda k=E: a.take(NT * k).rearrange("p (n e) -> p n e", n=NT)
    score, kept, rank, weight, rest = (tile8() for _ in range(5))
    gsum, grank = (tile8(E // 2) for _ in range(2))
    won = a.take(NT * E * (E - 1)).rearrange("p (n e d) -> p n e d", n=NT, e=E)
    gwon = a.take(NT * (E // 2) * (E // 2 - 1)).rearrange("p (n e d) -> p n e d", n=NT, e=E // 2)
    exT = a.take(SPAN)
    wsum, winv = a.take(NT), a.take(NT)
    parts = a.take(NT * PARTS * E, BF16).rearrange("p (n k e) -> p n k e", n=NT, k=PARTS)
    wT = a.take(N, BF16)
    silu = a.take(2 * SPAN).rearrange("p (k n) -> p k n", k=2)
    hid = a.take(3 * SPAN).rearrange("p (k n) -> p k n", k=3)
    HID = [0, 1, 2, 0, 1]
    USED = [0, -1, 1, 2, 3]
    yT = a.take(SPAN)
    assert a.at <= NORM_AT
    link_sem = sem(tag + "_vector_chain")
    HALVES = [range(0, NSPAN // 2), range(NSPAN // 2, NSPAN)]
    scored = sem(tag + "_scored")
    logits_ready, exT_ready, ex_ready = sem(tag + "_logits"), sem(tag + "_exT"), sem(tag + "_ex")
    parts_ready, wt_ready = sem(tag + "_parts_ready"), sem(tag + "_wt_ready")
    wT_zeroed, wT_ready = sem(tag + "_wT_zeroed"), sem(tag + "_wT_ready")
    gate_ready, up_ready, spread_ready = sem(tag + "_gate"), sem(tag + "_up"), sem(tag + "_spread")
    silu_ready, hid_ready = sem(tag + "_silu"), sem(tag + "_hid")
    prod_ready = sem(tag + "_prod")
    down_done, y_ready = sem(tag + "_down"), sem(tag + "_y")
    yt_ready, x_added = sem(tag + "_yt"), sem(tag + "_x")
    stats_ready, stored = sem(tag + "_stats"), sem(tag + "_stored")
    gate_ps = [b[0][:, 0:SPAN], b[0][:, SPAN:]]
    up_ps = [b[1][:, 0:SPAN], b[1][:, SPAN:]]
    spread_ps = [b[2][:, 0:SPAN], b[2][:, SPAN:]]
    down_ps, back_ps = b[3][:, 0:SPAN], b[3][:, SPAN:]
    logit_ps, ex_ps = b[2][:, 0:SPAN], b[2][:, SPAN:]
    wt_ps = back_ps.bitcast(BF16)

    with nc.Block() as block:
        @block.tensor
        def _(pe):
            def down(i, c, first):
                if c == NCH:
                    pe.wait_ge(prod_ready, i * HCH + HCH)
                else:
                    pe.wait_ge(hid_ready, i * NCH + c + 1)
                if c == 0 and not first:
                    pe.wait_ge(y_ready, i)
                mm = nc.tensor.matmul(down_ps, m.WD[:, c, :], hid[:, HID[c], :], start=(c == 0), stop=(c == NCH))
                if c == NCH:
                    mm.then_inc(down_done, 1)

            def turn_back(n):
                pe.wait_ge(y_ready, n)
                for k in range(TPS):
                    last = nc.tensor.transpose(back_ps[:, k * P:(k + 1) * P], yT[:, k * P:(k + 1) * P], m.ident[:, :])
                last.then_inc(yt_ready, 1)

            def products(i, c, again):
                x = m.xnT[:, bass.ds(i * SPAN, SPAN)]
                if again:
                    pe.wait_ge(silu_ready, i * HCH + USED[c])
                nc.tensor.matmul(gate_ps[c % 2], m.WG[:, c * P:(c + 1) * P], x, start=True, stop=True)\
                    .then_inc(gate_ready, 1)
                if again:
                    pe.wait_ge(prod_ready, i * HCH + USED[c])
                nc.tensor.matmul(up_ps[c % 2], m.WU[:, c * P:(c + 1) * P], x, start=True, stop=True)\
                    .then_inc(up_ready, 1)

            def spread(i, c, again):
                if again:
                    pe.wait_ge(hid_ready, i * NCH + (c - 1))
                nc.tensor.matmul(spread_ps[c % 2], m.sel[:, c * P:(c + 1) * P],
                                 wT[:, bass.ds(i * SPAN, SPAN)], start=True, stop=True)\
                    .then_inc(spread_ready, 1)

            def turn_weights(j):
                for k in range(TPS):
                    tile = parts[:, j * TPS + k, :, :].rearrange("p k e -> p (k e)")
                    last = nc.tensor.transpose(wt_ps[32 * j:32 * j + PARTS * E, k * P:(k + 1) * P], tile,
                                               m.identb[:, :])
                last.then_inc(wt_ready, 1)

            def span(i, first):
                for c in range(HCH):
                    again = not first or c >= 2
                    if again:
                        products(i, c, True)
                    if c < NCH:
                        spread(i, c, again)
                    if first and c == 4:
                        pe.wait_ge(parts_ready, 2)
                        for j in range(1, NSPAN):
                            turn_weights(j)
                    if c >= 1:
                        down(i, c - 1, first)
                    elif not first:
                        down(i - 1, NCH, False)
                    if c == 1 and not first:
                        turn_back(i)

            def logits(half):
                for i in HALVES[half]:
                    pe.wait_ge(s.xnT_ready, i + 1)
                    last = nc.tensor.matmul(logit_ps[32 * i:32 * (i + 1), :], m.gw[:, :],
                                            m.xnT[:, i * SPAN:(i + 1) * SPAN], start=True, stop=True)
                last.then_inc(logits_ready, 1)

            def turn_scores(half):
                pe.wait_ge(exT_ready, half + 1)
                if half:
                    pe.wait_ge(scored, half)
                rows = slice(64 * half, 64 * (half + 1))
                for k in range(TPS):
                    last = nc.tensor.transpose(ex_ps[:, k * P + 64 * half:k * P + 64 * (half + 1)],
                                               exT[rows, k * P:(k + 1) * P], m.ident[rows, rows])
                last.then_inc(ex_ready, 1)

            for i in range(normed, NSPAN // 2):
                norm_transpose(nc, m, s, pe, i)
            if tag == "f1":
                pe.wait_ge(m.gate_loaded, 16 * 2)
            logits(0)
            for i in HALVES[1]:
                norm_transpose(nc, m, s, pe, i)
            turn_scores(0)
            if tag == "f1":
                pe.wait_ge(m.ffn_loaded, 16 * FFN_DMAS)
            logits(1)
            products(0, 0, False)
            turn_scores(1)
            products(0, 1, False)
            pe.wait_ge(parts_ready, 1)
            turn_weights(0)
            pe.wait_ge(wT_ready, 1)
            span(0, True)
            pe.wait_ge(wT_ready, NSPAN)
            with pe.Fori(1, NSPAN) as i:
                span(i, False)
            down(NSPAN - 1, NCH, False)
            turn_back(NSPAN)
            if following is not None:
                for i in range(NSPAN // B):
                    norm_transpose(nc, m, following, pe, i)

        @block.scalar
        def _(act):
            def sigmoid(half):
                act.wait_ge(logits_ready, half + 1)
                rows = slice(64 * half, 64 * (half + 1))
                nc.scalar.activation(exT[rows, :], logit_ps[rows, :], ACT.Sigmoid).then_inc(exT_ready, 1)

            norm_root(nc, m, s, act, part)
            nc.scalar.activation(m.table[:, :], m.eps[:, :], ACT.Sigmoid)
            for i in range(normed, NSPAN):
                norm_last_tile(nc, m, s, act, i)
            for i in range(normed, NSPAN // 2):
                norm_take(nc, m, s, act, i)
            sigmoid(0)
            for i in HALVES[1]:
                norm_take(nc, m, s, act, i)
            sigmoid(1)

            def take_out(n):
                act.wait_ge(down_done, n)
                nc.scalar.activation(yT, down_ps, ACT.Copy, scale=0.5).then_inc(y_ready, 1)

            def take_weights(j):
                act.wait_ge(wt_ready, j + 1)
                nc.scalar.activation(wT[0:PARTS * E, j * SPAN:(j + 1) * SPAN], wt_ps[32 * j:32 * j + PARTS * E, 0:SPAN],
                                     ACT.Copy).then_inc(wT_ready, 1)

            def span(i, first):
                for c in range(HCH):
                    if first and c == 2:
                        act.wait_ge(wT_zeroed, 1)
                        take_weights(0)
                    act.wait_ge(gate_ready, i * HCH + c + 1)
                    if not first or c >= 2:
                        act.wait_ge(prod_ready, i * HCH + USED[c])
                    nc.scalar.activation(silu[:, c % 2, :], gate_ps[c % 2], ACT.Silu).then_inc(silu_ready, 1)
                    if c == 0 and not first:
                        take_out(i)

            span(0, True)
            for j in range(1, NSPAN):
                take_weights(j)
            with act.Fori(1, NSPAN) as i:
                span(i, False)
            if following is not None:
                nc.scalar.activation(m.table[:, :], m.eps[:, :], ACT.Sqrt)
                act.wait_ge(following.moments_ready, 1)
                norm_root(nc, m, following, act, 0)
            take_out(NSPAN)
            if following is not None:
                for i in range(NSPAN // B):
                    norm_last_tile(nc, m, following, act, i)
                for i in range(NSPAN // B):
                    norm_take(nc, m, following, act, i)

        if load is not None:
            @block.sync
            def _(sp):
                load(sp)

        if out is not None:
            @block.sync
            def _(sp):
                out_v = out.rearrange("b (n p) c -> p (b n) c", p=P)
                for i in range(NSPAN):
                    t = slice(i * TPS, (i + 1) * TPS)
                    sp.wait_ge(x_added, i + 1)
                    sp.dma_start(out_v[:, t, :], m.X[:, t, :]).then_inc(stored, 16)
                sp.wait_ge(stored, 16 * NSPAN)

        @block.gpsimd
        def _(pool):
            nc.gpsimd.memset(wT.bitcast(F32), 0.0).then_inc(wT_zeroed, 1)
            if beside is not None:
                pool.wait_ge(wT_zeroed, 1)
                beside(nc, m, sem, pool)

        @block.vector
        def _(dve):
            link = Chain(dve, link_sem)
            norm_vector(nc, m, s, dve, part)
            if tag == "f1":
                dve.wait_ge(m.gate_loaded, 16 * 2)

            def scores(half):
                dve.wait_ge(ex_ready, half + 1)
                ex = ex_ps.rearrange("p (k j e) -> p j k e", j=NSPAN, k=TPS)[:, :, :, 0:E]
                for j in HALVES[half]:
                    last = nc.vector.tensor_tensor(score[:, j * TPS:(j + 1) * TPS, :], ex[:, j],
                                                   m.gb[:, :].unsqueeze(1).to_broadcast([P, TPS, E]), ALU.add)
                last.then_inc(scored, 1)
                dve.wait_ge(scored, half + 1)

            def count_better(v, won, rank, n):
                for d in range(1, n):
                    nc.vector.tensor_tensor(won[:, :, d:n, d - 1], v[:, :, 0:n - d], v[:, :, d:n], ALU.is_ge)
                    last = nc.vector.tensor_tensor(won[:, :, 0:d, d - 1], v[:, :, n - d:n], v[:, :, 0:d], ALU.is_gt)
                link(last)
                link(nc.vector.tensor_reduce(rank, won, mybir.AxisListType.X, ALU.add))

            def pick_groups(t):
                link(nc.vector.tensor_tensor(gsum[:, t], score[:, t, 0:E:2], score[:, t, 1:E:2], ALU.add))
                count_better(gsum[:, t], gwon[:, t], grank[:, t], E // 2)
                for k in range(2):
                    last = nc.vector.scalar_tensor_tensor(kept[:, t, k:E:2], grank[:, t], 2.0, score[:, t, k:E:2],
                                                          ALU.is_lt, ALU.mult)
                link(last)

            def pick_experts(t):
                count_better(kept[:, t], won[:, t], rank[:, t], E)
                link(nc.vector.scalar_tensor_tensor(weight[:, t], rank[:, t], 2.0, score[:, t], ALU.is_lt, ALU.mult))

            def weigh(t):
                link(nc.vector.tensor_reduce(wsum[:, t], weight[:, t], mybir.AxisListType.X, ALU.add))
                link(nc.vector.tensor_scalar(wsum[:, t], wsum[:, t], 1e-20, None, ALU.add))
                link(nc.vector.reciprocal(winv[:, t], wsum[:, t]))
                inv = winv[:, t].unsqueeze(2).to_broadcast([P, t.stop - t.start, E])
                link(nc.vector.scalar_tensor_tensor(weight[:, t], weight[:, t], 2.5, inv, ALU.mult, ALU.mult))
                link(nc.vector.tensor_copy(parts[:, t, 0, :], weight[:, t]))
                link(nc.vector.tensor_tensor(rest[:, t], weight[:, t], parts[:, t, 0, :], ALU.subtract))
                link(nc.vector.tensor_copy(parts[:, t, 1, :], rest[:, t]))
                nc.vector.tensor_tensor(parts[:, t, 2, :], rest[:, t], parts[:, t, 1, :], ALU.subtract)\
                    .then_inc(parts_ready, 1)

            def product(i, c):
                dve.wait_ge(silu_ready, i * HCH + c + 1)
                dve.wait_ge(up_ready, i * HCH + c + 1)
                nc.vector.tensor_tensor(hid[:, HID[c], :], silu[:, c % 2, :], up_ps[c % 2], ALU.mult)\
                    .then_inc(prod_ready, 1)

            now, later = slice(0, TPS), slice(TPS, NT)
            scores(0)
            pick_groups(now)
            pick_experts(now)
            scores(1)
            weigh(now)
            product(0, 0)

            def add_to_x(n):
                dve.wait_ge(yt_ready, n)
                xs = m.X[:, bass.ds((n - 1) * TPS, TPS), :].rearrange("p n c -> p (n c)")
                nc.vector.tensor_tensor(xs, back_ps, xs, ALU.add).then_inc(x_added, 1)
                if out is None:
                    dve.wait_ge(x_added, n)
                    span_stats(nc, m, n - 1, stats_ready)

            def span(i, first):
                for c in range(HCH):
                    h = hid[:, HID[c], :]
                    if not (first and c == 0):
                        product(i, c)
                    if c < NCH:
                        dve.wait_ge(prod_ready, i * HCH + c + 1)
                        dve.wait_ge(spread_ready, i * NCH + c + 1)
                        nc.vector.tensor_tensor(h, h, spread_ps[c % 2], ALU.mult).then_inc(hid_ready, 1)
                    if first and c == 0:
                        pick_groups(later)
                    if first and c == 1:
                        pick_experts(later)
                    if first and c == 2:
                        weigh(later)
                    if c == 2 and not first:
                        add_to_x(i)

            span(0, True)
            with dve.Fori(1, NSPAN) as i:
                span(i, False)
            if following is not None:
                for n in range(NSPAN // B):
                    last = span_moments(nc, m, dve, n, stats_ready)
                last.then_inc(following.moments_ready, 1)
                for n in range(NSPAN // B, NSPAN - 1):
                    span_moments(nc, m, dve, n, stats_ready)
                norm_vector(nc, m, following, dve, 0)
            add_to_x(NSPAN)
            if out is None:
                span_moments(nc, m, dve, NSPAN - 1, stats_ready)


def load_quad(nc, m, sp, q_dram, k_dram, q, buf):
    rows = lambda v, lo, hi: v[bass.ds(q * G, G), lo * D:hi * D, :].rearrange("h r t -> r h t")
    for turn in range(PARTS):
        at = turn * PARTS
        sp.dma_start(m.Q[buf][at * D:(at + PARTS) * D, :, :], rows(q_dram, 0, PARTS)).then_inc(m.qk_loaded[buf], 16)
        for lo, hi in ((turn, PARTS), (0, turn)):
            if lo < hi:
                sp.dma_start(m.K[buf][at * D:(at + hi - lo) * D, :, :], rows(k_dram, lo, hi))\
                    .then_inc(m.qk_loaded[buf], 16)
                at += hi - lo


LOAD_DMAS = 3 * PARTS - 1


def project_qkv(nc, m, sem, s, q_dram, k_dram):
    a = Arena(m)
    banks = [m.psum[i // 2][:, (i % 2) * SPAN:(i % 2 + 1) * SPAN] for i in range(8)]
    full, rest = {w: a.take(N) for w in "qk"}, {w: a.take(N) for w in "qk"}
    late = Arena(m, (2 + 1) * G * T + G * SPAN + 2 * G * T)
    parts = {w: [late.take(N, BF16) for _ in range(PARTS)] for w in "qk"}
    sign, neg, qbias = a.take(1), a.take(1), a.take(1)
    ksum, kmean = a.take(NSPAN), a.take(B)
    assert a.at <= NORM_AT
    spb = NSPAN // B
    chain, sign_ready, k_done = sem("qkv_chain"), sem("sign_ready"), sem("k_with_bias")
    q_rows, k_rows, v_rows = sem("q_rows"), sem("k_rows"), sem("v_rows")
    v_out, quad0_stored = sem("v_out"), sem("quad0_stored")
    full_ready = {w: sem(w + "_full") for w in "qk"}
    high, middle, rest_ready = ({w: sem(f"{w}_{n}") for w in "qk"} for n in ("high", "middle", "rest"))
    low = {w: sem(w + "_low") for w in "qk"}
    of = lambda v, b: v[:, b * T:(b + 1) * T]
    def store_parts(sp, b, h0, h1, done):
        for n, ready in enumerate((high, middle, low)):
            for w, dram in (("q", q_dram), ("k", k_dram)):
                sp.wait_ge(ready[w], b + 1)
                rows = dram[b * N_HEAD + h0:b * N_HEAD + h1, n * D:(n + 1) * D, :]
                sp.dma_start(rows, of(parts[w][n], b)[h0 * D:h1 * D, :]).then_inc(done, 16)

    with nc.Block() as block:
        @block.tensor
        def _(pe):
            def project(w, b, rows, read):
                n = "qk".index(w)
                for i in range(spb * b, spb * (b + 1)):
                    if b:
                        pe.wait_ge(*read)
                    nc.tensor.matmul(banks[2 * n + i % spb], m.WA[:, n * C:(n + 1) * C],
                                     m.xnT[:, i * SPAN:(i + 1) * SPAN], start=True, stop=True).then_inc(rows, 1)

            def values(b):
                for i in range(spb * b, spb * (b + 1)):
                    if b:
                        pe.wait_ge(v_out, i - spb + 1)
                    for k in range(TPS):
                        t = i * TPS + k
                        last = nc.tensor.matmul(banks[6 + i % spb][:, k * P:(k + 1) * P],
                                                m.xnT[:, t * P:(t + 1) * P], m.WA[:, 2 * C:], start=True, stop=True)
                    last.then_inc(v_rows, 1)

            for b in range(B):
                if b:
                    for i in range(spb * b, spb * (b + 1)):
                        norm_transpose(nc, m, s, pe, i)
                    values(b - 1)
                pe.wait_ge(s.xnT_ready, spb * (b + 1))
                project("k", b, k_rows, (k_done, spb))
                project("q", b, q_rows, (full_ready["q"], spb))
            values(B - 1)

        @block.scalar
        def _(act):
            norm_root(nc, m, s, act, 1)

            def q_full(b):
                for i in range(spb * b, spb * (b + 1)):
                    act.wait_ge(q_rows, i + 1)
                    nc.scalar.activation(full["q"][:, i * SPAN:(i + 1) * SPAN], banks[i % spb], ACT.Identity,
                                         bias=qbias[:, 0:1], scale=sign[:, 0:1]).then_inc(full_ready["q"], 1)

            def high_part(w, b):
                act.wait_ge(full_ready[w], spb * (b + 1) if w == "q" else b + 1)
                nc.scalar.activation(of(parts[w][0], b), of(full[w], b), ACT.Copy).then_inc(high[w], 1)

            def middle_part(w, b):
                act.wait_ge(rest_ready[w], b + 1)
                nc.scalar.activation(of(parts[w][1], b), of(rest[w], b), ACT.Copy).then_inc(middle[w], 1)

            for i in range(spb, NSPAN):
                norm_last_tile(nc, m, s, act, i)
            act.wait_ge(sign_ready, 1)
            q_full(0)
            high_part("q", 0)
            high_part("k", 0)
            for i in range(spb, NSPAN):
                norm_take(nc, m, s, act, i)
            middle_part("q", 0)
            middle_part("k", 0)
            q_full(1)
            high_part("q", 1)
            high_part("k", 1)
            middle_part("q", 1)
            middle_part("k", 1)

        def rest_part(e, w, b):
            e_wait, op = e
            e_wait(high[w], b + 1)
            op(of(rest[w], b), of(full[w], b), of(parts[w][0], b), ALU.subtract).then_inc(rest_ready[w], 1)

        def low_part(e, w, b):
            e_wait, op = e
            e_wait(middle[w], b + 1)
            op(of(parts[w][2], b), of(rest[w], b), of(parts[w][1], b), ALU.subtract).then_inc(low[w], 1)

        @block.vector
        def _(dve):
            link = Chain(dve, chain)
            link(nc.vector.tensor_scalar(sign, m.gain[:, :], 0.0, None, ALU.is_gt))
            link(nc.vector.tensor_scalar(neg, m.gain[:, :], 0.0, None, ALU.is_lt))
            link(nc.vector.tensor_tensor(sign, sign, neg, ALU.subtract))
            nc.vector.tensor_tensor(qbias, m.bqk[:, 0:1], sign, ALU.mult).then_inc(sign_ready, 1)
            norm_vector(nc, m, s, dve, 1)

            def k_full(b):
                for i in range(spb * b, spb * (b + 1)):
                    dve.wait_ge(k_rows, i + 1)
                    nc.vector.tensor_scalar(full["k"][:, i * SPAN:(i + 1) * SPAN], banks[2 + i % spb], m.bqk[:, 1:2],
                                            0.0, ALU.add, ALU.add, accum_out=ksum[:, i:i + 1]).then_inc(k_done, 1)
                dve.wait_ge(k_done, spb * (b + 1))
                link(nc.vector.tensor_tensor(kmean[:, b:b + 1], ksum[:, spb * b:spb * b + 1],
                                             ksum[:, spb * b + 1:spb * b + 2], ALU.add))
                link(nc.vector.tensor_scalar(kmean[:, b:b + 1], kmean[:, b:b + 1], -1.0 / T, None, ALU.mult))
                nc.vector.tensor_scalar(of(full["k"], b), of(full["k"], b), kmean[:, b:b + 1], None, ALU.add)\
                    .then_inc(full_ready["k"], 1)

            def v_full(b):
                for i in range(spb * b, spb * (b + 1)):
                    dve.wait_ge(v_rows, i + 1)
                    n0 = i * TPS % NB
                    qn = lambda v: v.rearrange("p n (q c) -> p q n c", q=QPB)
                    nc.vector.tensor_tensor(m.V[:, b * QPB:(b + 1) * QPB, n0:n0 + TPS, :],
                                            qn(banks[6 + i % spb].rearrange("p (n c) -> p n c", n=TPS)),
                                            qn(m.bv[:, :].unsqueeze(1).to_broadcast([P, TPS, C])),
                                            ALU.add).then_inc(v_out, 1)

            e = (dve.wait_ge, nc.vector.tensor_tensor)
            k_full(0)
            rest_part(e, "q", 0)
            rest_part(e, "k", 0)
            low_part(e, "k", 0)
            v_full(0)
            k_full(1)
            rest_part(e, "k", 1)
            v_full(1)
            low_part(e, "k", 1)

        @block.gpsimd
        def _(pool):
            pool.wait_ge(s.xn_ready, NT - NSPAN)
            pool.wait_ge(s.xn_ready_a, NSPAN)
            nc.gpsimd.tensor_tensor(m.X[:, :, :], m.X[:, :, :], m.bp[:, :].unsqueeze(1).to_broadcast([P, NT, C]),
                                    ALU.add)
            e = (pool.wait_ge, nc.gpsimd.tensor_tensor)
            low_part(e, "q", 0)
            rest_part(e, "q", 1)
            low_part(e, "q", 1)

        @block.sync
        def _(sp):
            store_parts(sp, 0, 0, G, quad0_stored)
            sp.wait_ge(quad0_stored, 16 * 2 * PARTS)
            load_quad(nc, m, sp, q_dram, k_dram, 0, 0)

    def store_rest(sp):
        store_parts(sp, 0, G, N_HEAD, m.parts_stored)
        store_parts(sp, 1, 0, N_HEAD, m.parts_stored)

    return store_rest


def attention(nc, m, sem, q_dram, k_dram, att_dram, store_rest, following):
    a = Arena(m)
    Q, K, masks, Vq = m.Q, m.K, m.masks, m.Vq
    wide_tile = lambda: a.take(G * T).rearrange("p (g t) -> p g t", g=G)
    half_tile = lambda: a.take(G * SPAN).rearrange("p (g t) -> p g t", g=G)
    relus, powers = [wide_tile() for _ in range(2)], [wide_tile() for _ in range(NR - 1)] + [half_tile()]
    relus = [relus[0], relus[1], relus[0], relus[1], half_tile()]
    Y = lambda r, g: relus[r][:, g, :]
    Z = lambda r, g: powers[r][:, g, :]
    off = lambda r: SPAN if r == NR - 1 else 0
    sums = a.take(T)
    tiles = m.psum[0:3]
    acc = m.psum[3]

    lower_ready, upper_ready = sem("lower_ready"), sem("upper_ready")
    relu_done, square_done = sem("relu_done"), sem("square_done")
    upper_v, upper_a = sem("upper_summed_vector"), sem("upper_summed_scalar")
    fourth_p, fourth_a = sem("fourth_gpsimd"), sem("fourth_scalar")
    sums_out, sums_stored = sem("sums_out"), sem("sums_stored")
    power_summed, relu_summed = sem("power_round_summed"), sem("relu_round_summed")
    sums_free = sem("sums_free")
    vq_ready = sem("vq_ready")
    merge = Merge(nc, m, sem, following)
    steps = [(r, g) for r in range(NR) for g in range(G)]
    count = lambda who, upto, inclusive=True: sum(who(r, g) for r, g in steps[:steps.index(upto) + inclusive])
    all_of = lambda who: sum(who(r, g) for r, g in steps)
    by_v, by_a = upper_by_vector, lambda r, g: not upper_by_vector(r, g)
    sq_p, sq_a = square_by_gpsimd, lambda r, g: not square_by_gpsimd(r, g)
    NV, NA, NP4, NA4 = all_of(by_v), all_of(by_a), all_of(sq_p), all_of(sq_a)
    order = []
    for r, g in steps:
        order += [("both", r, g)] if r == NR - 1 else [("lower", r, g), ("upper", r, g)]
    assert len(order) % 3 == 0
    slot = {}
    for n, (kind, r, g) in enumerate(order):
        for k in ("lower", "upper") if kind == "both" else (kind,):
            slot[k, r, g] = n % 3

    def quads(engine, body):
        body(0, 0, 1)
        with engine.Fori(0, NQUAD // 2 - 1) as pair:
            body(2 * pair + 1, 1, pair + 1)
            body(2 * pair + 2, 0, pair + 2)
        body(NQUAD - 1, 1, NQUAD // 2)

    first_quad = lambda q: isinstance(q, int) and q == 0
    last_quad = lambda q: isinstance(q, int) and q == NQUAD - 1

    with nc.Block() as block:
        @block.sync
        def _(sp):
            def store(n):
                sp.wait_ge(sums_out, n)
                for g in range(G):
                    head = att_dram[bass.ds((n - 1) * G + g, 1)].rearrange("h k d t -> (h k d) t")
                    sp.dma_start(head, sums[32 * g:32 * (g + 1), :]).then_inc(sums_stored, 16)
                sp.wait_ge(sums_stored, 16 * G * n)
                sp.sem_inc(sums_free, 1)

            def body(q, buf, nth):
                if not last_quad(q):
                    if not first_quad(q):
                        sp.wait_ge(upper_ready, q * STEPS)
                    load_quad(nc, m, sp, q_dram, k_dram, q + 1, 1 - buf)
                if not first_quad(q):
                    store(q)

            sp.sem_inc(sums_free, 1)
            sp.wait_ge(m.qk_loaded[0], 16 * LOAD_DMAS)
            store_rest(sp)
            sp.wait_ge(m.parts_stored, 16 * 4 * PARTS)
            quads(sp, body)
            merge.load(sp, att_dram)
            sp.wait_ge(sums_out, NQUAD)
            merge.load_last_quad(sp, sums, range(G // 2))

        @block.tensor
        def _(pe):
            def wait_tile(q, r, g, kind):
                n = next(i for i, (k, rr, gg) in enumerate(order) if (rr, gg) == (r, g) and k in (kind, "both"))
                back = n - 3
                if back < 0 and first_quad(q):
                    return
                k, rr, gg = order[back]
                qq = q - 1 if back < 0 else q
                at = (rr, gg)
                if k in ("lower", "both"):
                    pe.wait_ge(relu_done, qq * STEPS + steps.index(at) + 1)
                if k in ("upper", "both"):
                    if by_v(*at):
                        pe.wait_ge(upper_v, qq * NV + count(by_v, at))
                    else:
                        pe.wait_ge(upper_a, qq * NA + count(by_a, at))

            def fill(q, par, r, g, kind):
                left, right = (K, Q) if kind == "lower" else (Q, K)
                bank = tiles[slot[kind, r, g]]
                shift = -SPAN if (r == NR - 1 and kind == "upper") else 0
                for blk, col, seq in tile_blocks(r):
                    for lo, hi in bank_pieces(col, col + width(blk)):
                        s0 = seq + lo - col
                        last = nc.tensor.matmul(bank[:, lo + shift:hi + shift], left[par][:, g, blk * P:(blk + 1) * P],
                                                right[par][:, g, s0:s0 + hi - lo], start=True, stop=True)
                last.then_inc(lower_ready if kind == "lower" else upper_ready, 1)

            def pieces(q, what, r):
                skip = P if what == "relu" else 0
                cut = [(blk, lo, hi, seq - col) for blk, col, seq in tile_blocks(r)
                       for lo, hi in bank_pieces(col + skip, col + width(blk))]
                return [(q, what, r, n == 0, n == len(cut) - 1, *c) for n, c in enumerate(cut)]

            def add_piece(q, what, r, first, last, blk, lo, hi, to_seq):
                if first and what == "relu":
                    pe.wait_ge(relu_done, q * STEPS + (r + 1) * G)
                    if r == 0 and not first_quad(q):
                        pe.wait_ge(sums_out, q)
                if first and what == "power":
                    pe.wait_ge(fourth_p, q * NP4 + count(sq_p, (r, G - 1)))
                    pe.wait_ge(fourth_a, q * NA4 + count(sq_a, (r, G - 1)))
                    if r == 0:
                        pe.wait_ge(vq_ready, q + 1)
                s0 = lo + to_seq
                start = what == "relu" and r == 0
                stop = what == "power" and (r == NR - 1 or (r == NR - 2 and s0 < SPAN))
                for g in range(G):
                    src = (Z if what == "power" else Y)(r, g)[:, lo - off(r):hi - off(r)]
                    w = Vq[:, blk, g, :] if what == "power" else m.ones_rows[:, :]
                    mm = nc.tensor.matmul(acc[32 * g:32 * (g + 1), s0:s0 + hi - lo], w, src, start=start,
                                          stop=stop, skip_group_check=True)
                if last:
                    mm.then_inc(relu_summed if what == "relu" else power_summed, 1)

            def plan(q, r):
                last = [] if first_quad(q) else [q - 1]
                some = lambda quad, what, rr: [x for p in quad for x in pieces(p, what, rr)]
                if r == 1:
                    return [[], some(last, "power", 4), [], some([q], "relu", 0)]
                work = {0: some(last, "relu", 3) + some(last, "power", 3) + some(last, "relu", 4),
                        2: some([q], "power", 0) + some([q], "relu", 1),
                        3: some([q], "power", 1) + some([q], "relu", 2),
                        4: some([q], "power", 2)}[r]
                return [work[g * len(work) // G:(g + 1) * len(work) // G] for g in range(G)]

            def body(q, buf, nth):
                pe.wait_ge(m.qk_loaded[buf], nth * (16 * LOAD_DMAS))
                for r, g in steps:
                    for kind in ("lower", "upper"):
                        if kind == "lower" or r < NR - 1:
                            wait_tile(q, r, g, kind)
                        fill(q, buf, r, g, kind)
                    for piece in plan(q, r)[g]:
                        add_piece(*piece)

            quads(pe, body)
            pe.wait_ge(relu_done, NQUAD * STEPS)
            pe.wait_ge(upper_v, NQUAD * NV)
            pe.wait_ge(upper_a, NQUAD * NA)
            merge.turn_upper(pe, 0)
            for what, r in (("relu", 3), ("power", 3), ("relu", 4)):
                for piece in pieces(NQUAD - 1, what, r):
                    add_piece(*piece)
            merge.turn_upper(pe, 1)
            for piece in pieces(NQUAD - 1, "power", 4):
                add_piece(*piece)
            merge.tensor(pe, sums, sums_out, NQUAD)

        @block.vector
        def _(dve):
            def body(q, buf, nth):
                for r, g in steps:
                    lo, hi = tile_low(r), T
                    before = {0: -3, 1: -2, 2: 0, 3: 1, 4: -1}[r]
                    if r in (2, 3) or not first_quad(q):
                        dve.wait_ge(relu_summed, q * NR + before + 1)
                        dve.wait_ge(square_done, (q * NR + before) * G + g + 1)
                    if first_quad(q) and (r, g) == (NR - 1, 0):
                        dve.wait_ge(m.parts_stored, 16 * 4 * PARTS)
                    dve.wait_ge(lower_ready, q * STEPS + r * G + g + 1)
                    mask = masks[:, 0, 0:SPAN] if r == NR - 1 else masks[:, r, lo:hi]
                    nc.vector.scalar_tensor_tensor(Y(r, g)[:, lo - off(r):hi - off(r)],
                                                   tiles[slot["lower", r, g]][:, lo:hi], 0.0, mask,
                                                   ALU.max, ALU.mult).then_inc(relu_done, 1)
                    if by_v(r, g):
                        dve.wait_ge(upper_ready, q * STEPS + r * G + g + 1)
                        shift = -SPAN if r == NR - 1 else 0
                        for blk, col, seq in tile_blocks(r):
                            src = tiles[slot["upper", r, g]][:, col + shift:col + width(blk) + shift]
                            last = nc.vector.tensor_scalar(src, src, 0.0, 0.0, ALU.max, ALU.add,
                                                           accum_out=m.upper[:, blk, bass.ds(q * G + g + N_HEAD, 1)])
                        last.then_inc(upper_v, 1)
            quads(dve, body)
            merge.vector(dve)

        @block.scalar
        def _(act):
            def evacuate(n):
                act.wait_ge(power_summed, n * NR)
                act.wait_ge(sums_free, n)
                nc.scalar.activation(sums, acc[:, :], ACT.Copy).then_inc(sums_out, 1)

            def body(q, buf, nth):
                for r, g in steps:
                    if (r, g) == (1, 2) and not first_quad(q):
                        evacuate(q)
                    n = q * STEPS + r * G + g + 1
                    if by_a(r, g):
                        act.wait_ge(upper_ready, n)
                        shift = -SPAN if r == NR - 1 else 0
                        for blk, col, seq in tile_blocks(r):
                            src = tiles[slot["upper", r, g]][:, col + shift:col + width(blk) + shift]
                            last = nc.scalar.activation(src, src, ACT.Relu,
                                                        accum_out=m.upper[:, blk, bass.ds(q * G + g + N_HEAD, 1)])
                        last.then_inc(upper_a, 1)
                    z = Z(r, g)[:, tile_low(r) - off(r):T - off(r)]
                    if not first_quad(q):
                        act.wait_ge(power_summed, (q - 1) * NR + r + 1)
                    elif (r, g) == (NR - 2, 0):
                        act.wait_ge(m.parts_stored, 16 * 4 * PARTS)
                    act.wait_ge(relu_done, n)
                    nc.scalar.activation(z, Y(r, g)[:, tile_low(r) - off(r):T - off(r)], ACT.Square)\
                        .then_inc(square_done, 1)
                    if sq_a(r, g):
                        act.wait_ge(square_done, n)
                        nc.scalar.activation(z, z, ACT.Square).then_inc(fourth_a, 1)
            quads(act, body)
            evacuate(NQUAD)
            act.wait_ge(sums_out, NQUAD)
            merge.load_last_quad(act, sums, range(G // 2, G))
            merge.scalar(act)

        @block.gpsimd
        def _(pool):
            def copy_v(q):
                src = m.V[:, bass.ds(q, 1), :, :].rearrange("p q n (g d) -> p (q n) g d", g=G)
                nc.gpsimd.tensor_copy(Vq[:, :, :, 0:D], src).then_inc(vq_ready, 1)

            def body(q, buf, nth):
                for r, g in steps:
                    if (r, g) == (1, 0) and not first_quad(q):
                        pool.wait_ge(power_summed, q * NR)
                        copy_v(q)
                    if sq_p(r, g):
                        pool.wait_ge(square_done, q * STEPS + r * G + g + 1)
                        lo = tile_low(r) - off(r)
                        hi = T - off(r)
                        z = Z(r, g)[:, lo:hi]
                        nc.gpsimd.tensor_tensor(z, z, z, ALU.mult).then_inc(fourth_p, 1)
            copy_v(0)
            quads(pool, body)


class Merge:

    def __init__(self, nc, m, sem, following):
        self.nc, self.m, self.following = nc, m, following
        self.num = m.xnT
        self.num_loaded = [sem("num_loaded0"), sem("num_loaded1")]
        self.sums_loaded = [sem("merge_sums_loaded0"), sem("merge_sums_loaded1")]
        self.num_dmas = [1, 1 + G]
        self.upper_t, self.rden_ready, self.spread_ready = sem("upper_t"), sem("rden_ready"), sem("rden_spread")
        self.chain, self.att_ready, self.proj_ready = sem("merge_chain"), sem("att_ready"), sem("proj_ready")
        self.x_added, self.stats_ready = sem("attention_added"), sem("attention_stats")
        self.upper_ps = [m.psum[0][:, b * SPAN:b * SPAN + QT] for b in range(B)]
        self.spread_ps = [m.psum[1], m.psum[3]]
        self.proj_ps = [m.psum[2][:, 0:SPAN], m.psum[2][:, SPAN:], m.psum[1][:, 0:SPAN], m.psum[1][:, SPAN:]]
        self.den_ps = m.psum[0][:, SPAN + QT:]
        self.picked = sem("last_quad_picked")

    def load(self, sp, att_dram):
        m = self.m
        for b in range(B):
            heads = N_HEAD if b < B - 1 else N_HEAD - G
            v = att_dram[b * N_HEAD:b * N_HEAD + heads]
            for k, dst in ((2, m.low[b]), (1, m.den[b])):
                for n in range(QUARTERS):
                    row = n * HB + HEAD_ROW[b]
                    sp.dma_start(dst[row:row + heads, :], v[:, k, 0, n * QT:(n + 1) * QT])\
                        .then_inc(self.sums_loaded[b], 16)
            sp.dma_start(self.num[0:heads * D, b * T:(b + 1) * T], v[:, 0, :, :]).then_inc(self.num_loaded[b], 16)

    def load_last_quad(self, engine, sums, heads):
        b = B - 1
        for g in heads:
            at = (N_HEAD - G + g) * D
            engine.dma_start(self.num[at:at + D, b * T:], sums[32 * g:32 * g + D, :]).then_inc(self.num_loaded[b], 16)

    def turn_upper(self, pe, b):
        nc, m = self.nc, self.m
        per = NB // QUARTERS
        for i in range(NB):
            n, k = i // per, i % per
            last = nc.tensor.matmul(self.upper_ps[b][n * HB:(n + 1) * HB, k * P:(k + 1) * P],
                                    m.upper[:, i, b * HB:(b + 1) * HB], m.ident[:, :],
                                    start=True, stop=(b == 0), skip_group_check=True)
        last.then_inc(self.upper_t, 1)

    def tensor(self, pe, sums, sums_out, last_sums):
        nc, m = self.nc, self.m
        for b in range(B):
            pe.wait_ge(self.rden_ready, b + 1)
            for n in range(QUARTERS):
                last = nc.tensor.matmul(self.spread_ps[b][:, n * QT:(n + 1) * QT], m.spread[:, n, b, :], m.den[b][:, :],
                                        start=True, stop=True)
                if n % 2 == 1:
                    last.then_inc(self.spread_ready, 1)
            if b == 0:
                pe.wait_ge(sums_out, last_sums)
                for n in range(QUARTERS):
                    for k, into in ((0, self.den_ps), (1, self.upper_ps[B - 1])):
                        last = nc.tensor.matmul(into[n * HB:(n + 1) * HB, :], m.pick[:, k, :],
                                                sums[:, n * QT:(n + 1) * QT], start=(k == 0), stop=True,
                                                skip_group_check=True)
                last.then_inc(self.picked, 1)
            for i in range(b * NSPAN // B, (b + 1) * NSPAN // B):
                pe.wait_ge(self.att_ready, i + 1)
                for k in range(TPS):
                    t = i * TPS + k
                    last = nc.tensor.matmul(self.proj_ps[i][:, k * P:(k + 1) * P], self.num[:, t * P:(t + 1) * P],
                                            m.WP[:, :], start=True, stop=True)
                last.then_inc(self.proj_ready, 1)
        for i in range(NSPAN // B):
            norm_transpose(nc, m, self.following, pe, i)

    def scalar(self, act):
        nc, m = self.nc, self.m
        nc.scalar.activation(m.table[:, :], m.eps[:, :], ACT.Sqrt)
        act.wait_ge(self.following.moments_ready, 1)
        norm_root(nc, m, self.following, act, 0)
        for i in range(NSPAN // B):
            norm_last_tile(nc, m, self.following, act, i)
        for i in range(NSPAN // B):
            norm_take(nc, m, self.following, act, i)

    def vector(self, dve):
        nc, m = self.nc, self.m
        link = Chain(dve, self.chain)

        def invert(b):
            mad, den = m.low[b][:, :], m.den[b][:, :]
            dve.wait_ge(self.upper_t, b + 1)
            if b == B - 1:
                dve.wait_ge(self.picked, 1)
            dve.wait_ge(self.sums_loaded[b], 16 * 2 * QUARTERS)
            link(nc.vector.tensor_tensor(mad, self.upper_ps[b], mad, ALU.add))
            link(nc.vector.tensor_scalar(mad, mad, 1e-6 * T / 2, slope[:, 0:1], ALU.add, ALU.mult))
            link(nc.vector.tensor_tensor(mad, mad, mad, ALU.mult))
            link(nc.vector.tensor_tensor(mad, mad, mad, ALU.mult))
            link(nc.vector.scalar_tensor_tensor(den, mad, 1e-6, den, ALU.mult, ALU.add))
            if b == B - 1:
                link(nc.vector.tensor_tensor(den, self.den_ps, den, ALU.add))
            nc.vector.reciprocal(den, den).then_inc(self.rden_ready, 1)

        def divide(i):
            b = i * B // NSPAN
            dve.wait_ge(self.num_loaded[b], 16 * self.num_dmas[b])
            dve.wait_ge(self.spread_ready, i + 1)
            sl = slice(i * SPAN, (i + 1) * SPAN)
            rd = self.spread_ps[i // 2][:, (i % 2) * SPAN:(i % 2 + 1) * SPAN]
            nc.vector.tensor_tensor(self.num[:, sl], self.num[:, sl], rd, ALU.mult).then_inc(self.att_ready, 1)

        def add_to_x(i):
            dve.wait_ge(self.proj_ready, i + 1)
            xs = m.X[:, i * TPS:(i + 1) * TPS, :].rearrange("p n c -> p (n c)")
            nc.vector.tensor_tensor(xs, self.proj_ps[i], xs, ALU.add).then_inc(self.x_added, 1)
            dve.wait_ge(self.x_added, i + 1)
            span_stats(nc, m, i, self.stats_ready)
            last = span_moments(nc, m, dve, i, self.stats_ready)
            if i == NSPAN // B - 1:
                last.then_inc(self.following.moments_ready, 1)

        slope = m.slope
        link(nc.vector.reciprocal(slope[:, :], m.gain[:, :]))
        link(nc.vector.tensor_scalar(slope[:, :], slope[:, :], 2.0 / T, None, ALU.mult))
        invert(0)
        divide(0)
        divide(1)
        invert(1)
        add_to_x(0)
        divide(2)
        add_to_x(1)
        divide(3)
        norm_vector(nc, m, self.following, dve, 0)
        add_to_x(2)
        add_to_x(3)


_INS = ['L0_attn_x', 'L0_attn_W_attn', 'L0_attn_b_attn', 'L0_attn_W_proj', 'L0_attn_b_proj', 'L0_attn_score_gain',
        'L0_ffn_gate_w', 'L0_ffn_gate_bias', 'L0_ffn_w_gate', 'L0_ffn_w_up', 'L0_ffn_w_down', 'L0_ffn_sw_gate',
        'L0_ffn_sw_up', 'L0_ffn_sw_down']


def kernel(**inputs):
    import numpy as np
    import concourse.bacc as bacc
    from concourse.bass_utils import run_bass_kernel_spmd

    nc = bacc.Bacc("TRN2", target_bir_lowering=False, num_devices=1)
    arrays, args = {}, []
    for name in _INS:
        a = np.ascontiguousarray(inputs[name])
        if a.ndim == 0:
            a = a.reshape(1, 1)
        arrays[f"in_{name}"] = a
        args.append(nc.dram_tensor(f"in_{name}", a.shape, mybir.dt.from_np(a.dtype), kind="ExternalInput").ap())
    out = nc.dram_tensor("out_x", (B, T, C), F32, kind="ExternalOutput").ap()
    build(nc, *args, out)
    r = run_bass_kernel_spmd(nc, [arrays], core_ids=[0])
    return r.results[0]["out_x"]
```
